# Optimizing a Trainium2 kernel written in Bass

```python
import numpy as np
import jax
import jax.numpy as jnp

def _softmax(x, axis=-1):
    return jax.nn.softmax(x, axis=axis)
def _gelu(x):
    return jax.nn.gelu(x, approximate=True)
def _silu(x):
    return jax.nn.silu(x)
def _sigmoid(x):
    return jax.nn.sigmoid(x)
def _layernorm(x, axis=-1, eps=1e-5):
    m = jnp.mean(x, axis=axis, keepdims=True)
    v = jnp.var(x, axis=axis, keepdims=True)
    return (x - m) / jnp.sqrt(v + eps)
def _scatter_add(tgt, idx, src, axis=0):
    return tgt.at[idx].add(src)
def _segment_sum(src, seg, n):
    return jax.ops.segment_sum(src, seg, n)

kernel_name = 'mk_conv_attn_hybrid_d2_conv_nchw384_68fdc5'

def setup_inputs(seed: int = 0):
    np.random.seed(seed)
    _w = jnp.asarray
    def _rec_inputs():
        import jax
        import jax.numpy as jnp
        _gk = jax.random.key(seed)
        x = -0.001003 + 1 * jax.random.normal(jax.random.fold_in(_gk, 1), (4, 384, 32, 32), jnp.float32)
        return x
    x = _rec_inputs()
    def _L0_conv_setup():
        import jax, jax.numpy as jnp
        import numpy as np
        D_MODEL = 192
        D_STATE = 16
        SSM_RATIO = 2.0
        D_INNER = int(SSM_RATIO * D_MODEL)
        DT_RANK = int(np.ceil(D_MODEL / 16))
        K_GROUP = 4
        BATCH, HH, WW = (4, 32, 32)
        DT_MIN, DT_MAX = (0.001, 0.1)
        LN_EPS = 1e-05

        def _cross_scan(x):
            B, D, H, W = x.shape
            x0 = x.reshape(B, D, H * W)
            x1 = jnp.transpose(x, (0, 1, 3, 2)).reshape(B, D, H * W)
            return jnp.stack([x0, x1, x0[..., ::-1], x1[..., ::-1]], axis=1)

        def _cross_merge(ys, H, W):
            B, K, D, L = ys.shape
            y0 = ys[:, 0]
            y2 = ys[:, 2][..., ::-1]
            yt = ys[:, 1] + ys[:, 3][..., ::-1]
            yt = jnp.transpose(yt.reshape(B, D, W, H), (0, 1, 3, 2)).reshape(B, D, L)
            return y0 + y2 + yt

        def _selective_scan(u, dt, A, Bs, Cs):
            dt_l = jnp.moveaxis(dt, -1, 0)
            u_l = jnp.moveaxis(u, -1, 0)
            B_l = jnp.moveaxis(Bs, -1, 0)
            C_l = jnpp_move = jnp.moveaxis(Cs, -1, 0)

            def step(h, inp):
                dtt, ut, bt, ct = inp
                dA = jnp.exp(dtt[..., None] * A)
                h = h * dA + (dtt * ut)[..., None] * bt[:, :, None, :]
                y = jnp.einsum('bkdn,bkn->bkd', h, ct)
                return (h, y)
            h0 = jnp.zeros(u.shape[:3] + (A.shape[-1],), dtype=u.dtype)
            _, ys = jax.lax.scan(step, h0, (dt_l, u_l, B_l, C_l))
            return jnp.moveaxis(ys, 0, -1)
        key = jax.random.key(seed)
        ks = jax.random.split(key, 6)
        x = jax.random.normal(ks[0], (BATCH, D_INNER, HH, WW), dtype=jnp.float32)
        x_proj_weight = jax.random.normal(ks[1], (K_GROUP, DT_RANK + 2 * D_STATE, D_INNER), dtype=jnp.float32) * D_INNER ** (-0.5)
        dt_projs_weight = jax.random.normal(ks[2], (K_GROUP, D_INNER, DT_RANK), dtype=jnp.float32) * DT_RANK ** (-0.5)
        dt = jnp.exp(jax.random.uniform(ks[3], (K_GROUP, D_INNER)) * (np.log(DT_MAX) - np.log(DT_MIN)) + np.log(DT_MIN))
        dt = jnp.clip(dt, 0.0001, None)
        dt_projs_bias = dt + jnp.log(-jnp.expm1(-dt))
        A = jnp.tile(jnp.arange(1, D_STATE + 1, dtype=jnp.float32)[None, :], (K_GROUP * D_INNER, 1))
        A_logs = jnp.log(A)
        Ds = jnp.ones((K_GROUP * D_INNER,), dtype=jnp.float32)
        ln_weight = jnp.ones((D_INNER,), dtype=jnp.float32)
        ln_bias = jnp.zeros((D_INNER,), dtype=jnp.float32)
        return {'x': x, 'x_proj_weight': x_proj_weight, 'dt_projs_weight': dt_projs_weight, 'dt_projs_bias': dt_projs_bias, 'A_logs': A_logs, 'Ds': Ds, 'ln_weight': ln_weight, 'ln_bias': ln_bias}
    _L0_conv_all = _L0_conv_setup()
    _L0_conv_in = {k: v for k, v in _L0_conv_all.items() if k in ('x_proj_weight', 'dt_projs_weight', 'dt_projs_bias', 'A_logs', 'Ds', 'ln_weight', 'ln_bias', )}
    del _L0_conv_all

    def _L1_attn_setup():
        import jax, jax.numpy as jnp
        import numpy as np
        N_EMBD = 384
        BLOCK_SIZE = 256
        HEAD_SIZE = 384
        B, T = (512, 256)
        key = jax.random.key(seed)
        k1, k2, k3, k4 = jax.random.split(key, 4)
        scale = 1.0 / np.sqrt(N_EMBD)
        return {'x': jax.random.normal(k1, (B, T, N_EMBD), dtype=jnp.float32), 'Wq': jax.random.normal(k2, (N_EMBD, HEAD_SIZE), dtype=jnp.float32) * scale, 'Wk': jax.random.normal(k3, (N_EMBD, HEAD_SIZE), dtype=jnp.float32) * scale, 'Wv': jax.random.normal(k4, (N_EMBD, HEAD_SIZE), dtype=jnp.float32) * scale}
    _L1_attn_all = _L1_attn_setup()
    _L1_attn_in = {k: v for k, v in _L1_attn_all.items() if k in ('Wq', 'Wk', 'Wv', )}
    del _L1_attn_all

    def _L1_ffn_setup():
        import jax, jax.numpy as jnp
        import numpy as np
        NUM_EXPERTS = 4
        TOP_K = 2
        DIM = 384
        HID = 4 * DIM
        key = jax.random.key(seed)
        ks = jax.random.split(key, 5)
        B, S = (16, 2048)
        scale_in = 1.0 / np.sqrt(DIM)
        scale_hid = 1.0 / np.sqrt(HID)
        return {'x': jax.random.normal(ks[0], (B, S, DIM), dtype=jnp.float32), 'gate_w': jax.random.normal(ks[1], (DIM, NUM_EXPERTS), dtype=jnp.float32) * scale_in, 'gate_b': jnp.zeros((NUM_EXPERTS,), dtype=jnp.float32), 'w1': jax.random.normal(ks[2], (NUM_EXPERTS, DIM, HID), dtype=jnp.float32) * scale_in, 'b1': jnp.zeros((NUM_EXPERTS, HID), dtype=jnp.float32), 'w2': jax.random.normal(ks[3], (NUM_EXPERTS, HID, DIM), dtype=jnp.float32) * scale_hid, 'b2': jnp.zeros((NUM_EXPERTS, DIM), dtype=jnp.float32)}
    _L1_ffn_all = _L1_ffn_setup()
    _L1_ffn_in = {k: v for k, v in _L1_ffn_all.items() if k in ('gate_w', 'gate_b', 'w1', 'b1', 'w2', 'b2', )}
    del _L1_ffn_all

    return {
        "x": x,
        "L0_conv_x_proj_weight": _L0_conv_in["x_proj_weight"],
        "L0_conv_dt_projs_weight": _L0_conv_in["dt_projs_weight"],
        "L0_conv_dt_projs_bias": _L0_conv_in["dt_projs_bias"],
        "L0_conv_A_logs": _L0_conv_in["A_logs"],
        "L0_conv_Ds": _L0_conv_in["Ds"],
        "L0_conv_ln_weight": _L0_conv_in["ln_weight"],
        "L0_conv_ln_bias": _L0_conv_in["ln_bias"],
        "L1_attn_Wq": _L1_attn_in["Wq"],
        "L1_attn_Wk": _L1_attn_in["Wk"],
        "L1_attn_Wv": _L1_attn_in["Wv"],
        "L1_ffn_gate_w": _L1_ffn_in["gate_w"],
        "L1_ffn_gate_b": _L1_ffn_in["gate_b"],
        "L1_ffn_w1": _L1_ffn_in["w1"],
        "L1_ffn_b1": _L1_ffn_in["b1"],
        "L1_ffn_w2": _L1_ffn_in["w2"],
        "L1_ffn_b2": _L1_ffn_in["b2"],
    }

def reference(x, L0_conv_x_proj_weight, L0_conv_dt_projs_weight, L0_conv_dt_projs_bias, L0_conv_A_logs, L0_conv_Ds, L0_conv_ln_weight, L0_conv_ln_bias, L1_attn_Wq, L1_attn_Wk, L1_attn_Wv, L1_ffn_gate_w, L1_ffn_gate_b, L1_ffn_w1, L1_ffn_b1, L1_ffn_w2, L1_ffn_b2):
    import jax
    import jax.numpy as jnp
    def _L0_conv_ref(x, x_proj_weight, dt_projs_weight, dt_projs_bias, A_logs, Ds, ln_weight, ln_bias):
        import jax, jax.numpy as jnp
        import numpy as np
        D_MODEL = 192
        D_STATE = 16
        SSM_RATIO = 2.0
        D_INNER = int(SSM_RATIO * D_MODEL)
        DT_RANK = int(np.ceil(D_MODEL / 16))
        K_GROUP = 4
        BATCH, HH, WW = (4, 32, 32)
        DT_MIN, DT_MAX = (0.001, 0.1)
        LN_EPS = 1e-05

        def _cross_scan(x):
            B, D, H, W = x.shape
            x0 = x.reshape(B, D, H * W)
            x1 = jnp.transpose(x, (0, 1, 3, 2)).reshape(B, D, H * W)
            return jnp.stack([x0, x1, x0[..., ::-1], x1[..., ::-1]], axis=1)

        def _cross_merge(ys, H, W):
            B, K, D, L = ys.shape
            y0 = ys[:, 0]
            y2 = ys[:, 2][..., ::-1]
            yt = ys[:, 1] + ys[:, 3][..., ::-1]
            yt = jnp.transpose(yt.reshape(B, D, W, H), (0, 1, 3, 2)).reshape(B, D, L)
            return y0 + y2 + yt

        def _selective_scan(u, dt, A, Bs, Cs):
            dt_l = jnp.moveaxis(dt, -1, 0)
            u_l = jnp.moveaxis(u, -1, 0)
            B_l = jnp.moveaxis(Bs, -1, 0)
            C_l = jnpp_move = jnp.moveaxis(Cs, -1, 0)

            def step(h, inp):
                dtt, ut, bt, ct = inp
                dA = jnp.exp(dtt[..., None] * A)
                h = h * dA + (dtt * ut)[..., None] * bt[:, :, None, :]
                y = jnp.einsum('bkdn,bkn->bkd', h, ct)
                return (h, y)
            h0 = jnp.zeros(u.shape[:3] + (A.shape[-1],), dtype=u.dtype)
            _, ys = jax.lax.scan(step, h0, (dt_l, u_l, B_l, C_l))
            return jnp.moveaxis(ys, 0, -1)
        B, D, H, W = x.shape
        K = x_proj_weight.shape[0]
        N = D_STATE
        R = dt_projs_weight.shape[-1]
        L = H * W
        xs = _cross_scan(x)
        x_dbl = jnp.einsum('bkdl,kcd->bkcl', xs, x_proj_weight)
        dts, Bs, Cs = (x_dbl[:, :, :R], x_dbl[:, :, R:R + N], x_dbl[:, :, R + N:])
        dts = jnp.einsum('bkrl,kdr->bkdl', dts, dt_projs_weight)
        A = -jnp.exp(A_logs.astype(jnp.float32)).reshape(K, D, N)
        dt = jax.nn.softplus(dts.astype(jnp.float32) + dt_projs_bias.astype(jnp.float32)[None, :, :, None])
        u = xs.astype(jnp.float32)
        Bs = Bs.astype(jnp.float32)
        Cs = Cs.astype(jnp.float32)
        ys = _selective_scan(u, dt, A, Bs, Cs)
        ys = ys + Ds.astype(jnp.float32).reshape(K, D)[None, :, :, None] * u
        y = _cross_merge(ys, H, W).reshape(B, D, H, W)
        yc = jnp.transpose(y, (0, 2, 3, 1))
        mu = jnp.mean(yc, axis=-1, keepdims=True)
        var = jnp.mean((yc - mu) ** 2, axis=-1, keepdims=True)
        yc = (yc - mu) * jax.lax.rsqrt(var + LN_EPS) * ln_weight + ln_bias
        y = jnp.transpose(yc, (0, 3, 1, 2)).astype(x.dtype)
        return jax.nn.gelu(y, approximate=False)

    def _L1_attn_ref(x, Wq, Wk, Wv):
        import jax, jax.numpy as jnp
        import numpy as np
        N_EMBD = 384
        BLOCK_SIZE = 256
        HEAD_SIZE = 384
        B, T = (512, 256)
        q = jnp.einsum('btc,ch->bth', x, Wq)
        k = jnp.einsum('btc,ch->bth', x, Wk)
        v = jnp.einsum('btc,ch->bth', x, Wv)
        scale = k.shape[-1] ** (-0.5)
        scores = jnp.einsum('bth,bsh->bts', q, k) * scale
        t = q.shape[1]
        causal = jnp.tril(jnp.ones((t, t), dtype=bool))
        scores = jnp.where(causal, scores, -jnp.inf)
        attn = jax.nn.softmax(scores, axis=-1)
        out = jnp.einsum('bts,bsh->bth', attn, v)
        return out

    def _L1_ffn_ref(x, gate_w, gate_b, w1, b1, w2, b2):
        import jax, jax.numpy as jnp
        import numpy as np
        NUM_EXPERTS = 4
        TOP_K = 2
        DIM = 384
        HID = 4 * DIM
        scores = jnp.einsum('bsd,de->bse', x, gate_w) + gate_b
        probs = jax.nn.softmax(scores, axis=-1)
        topk_vals, topk_idx = jax.lax.top_k(probs, TOP_K)
        mask = jnp.sum(jax.nn.one_hot(topk_idx, NUM_EXPERTS, dtype=probs.dtype), axis=-2)
        masked = probs * mask
        masked = masked / (jnp.sum(masked, axis=-1, keepdims=True) + 1e-09)
        h = jax.nn.gelu(jnp.einsum('bsd,edh->ebsh', x, w1) + b1[:, None, None, :], approximate=False)
        y = jnp.einsum('ebsh,ehd->ebsd', h, w2) + b2[:, None, None, :]
        out = jnp.einsum('bse,ebsd->bsd', masked, y)
        return out

    def _gn(v, G=32, eps=1e-5):
        B_, C_, H_, W_ = v.shape
        g = v.reshape(B_, G, C_ // G, H_, W_)
        m = jnp.mean(g, axis=(2, 3, 4), keepdims=True)
        s = jnp.var(g, axis=(2, 3, 4), keepdims=True)
        return ((g - m) / jnp.sqrt(s + eps)).reshape(v.shape)

    def _ln_c(v, eps=1e-6):
        m = jnp.mean(v, axis=1, keepdims=True)
        s = jnp.var(v, axis=1, keepdims=True)
        return (v - m) / jnp.sqrt(s + eps)

    def _ln_t(v, eps=1e-5):
        m = jnp.mean(v, axis=-1, keepdims=True)
        s = jnp.var(v, axis=-1, keepdims=True)
        return (v - m) / jnp.sqrt(s + eps)

    def _to_tokens(v):
        B_, C_, H_, W_ = v.shape
        return v.reshape(B_, C_, H_ * W_).transpose(0, 2, 1)
    def _from_tokens(t, like):
        B_, C_, H_, W_ = like.shape
        return t.transpose(0, 2, 1).reshape(B_, C_, H_, W_)

    x = x + _L0_conv_ref(_gn(x), L0_conv_x_proj_weight, L0_conv_dt_projs_weight, L0_conv_dt_projs_bias, L0_conv_A_logs, L0_conv_Ds, L0_conv_ln_weight, L0_conv_ln_bias)
    t = _to_tokens(x)
    t = t + _L1_attn_ref(_ln_t(t), L1_attn_Wq, L1_attn_Wk, L1_attn_Wv)
    t = t + _L1_ffn_ref(_ln_t(t), L1_ffn_gate_w, L1_ffn_gate_b, L1_ffn_w1, L1_ffn_b1, L1_ffn_w2, L1_ffn_b2)
    x = _from_tokens(t, x)
    return x


_drawn_inputs = setup_inputs


def setup_inputs(seed=0):
    import zlib

    import numpy as np

    out = dict(_drawn_inputs(seed))
    spreads = {'L0_conv_Ds': (1.0, 0.2),
     'L0_conv_ln_weight': (1.0, 0.2),
     'L0_conv_ln_bias': (0.0, 0.1),
     'L1_ffn_gate_b': (0.0, 0.1),
     'L1_ffn_b1': (0.0, 0.1),
     'L1_ffn_b2': (0.0, 0.1)}
    factors = {}
    for name, (base, spread) in spreads.items():
        noise = np.random.default_rng([zlib.crc32(name.encode()), seed]).standard_normal(out[name].shape)
        drawn = base * np.exp(spread * noise) if base else spread * noise
        out[name] = jnp.asarray(drawn.astype(out[name].dtype))
    for name, factor in factors.items():
        out[name] = (out[name] * factor).astype(out[name].dtype)
    return out
```

```python
from contextlib import ExitStack

import concourse.bass as bass
from concourse import mybir

F32 = mybir.dt.float32
BF16 = mybir.dt.bfloat16
ALU = mybir.AluOpType
ACT = mybir.ActivationFunctionType
AX = mybir.AxisListType

P = 128
NB, C, HH, WW = 4, 384, 32, 32
L = HH * WW
CT = C // P
HALF = 512
NH = L // HALF
K, N, R = 4, 16, 12
BC = 2 * N
TT = L // P
NE, HID = 4, 4 * C
PAIRS = HID // (2 * P)
GROUP = C // 32
EPS = 1e-5
MASKED = -1e30
RING = 3
SCALE = float(C) ** -0.5
DTB, ALOG, DSK, LNW, LNB, CHAN = 0, K, K + K * N, 2 * K + K * N, 2 * K + K * N + 1, 2 * K + K * N + 2


def build(nc, x, xpw, dtw, chan, wqkv, gate_w, gate_b, b1, b2, wpk, gmat, lower, out):
    with ExitStack() as ctx:
        def sb(name, shape, dt=F32):
            return ctx.enter_context(nc.sbuf_tensor(name, shape, dt))

        def sem(name):
            return ctx.enter_context(nc.semaphore(name))

        u = sb("u", [P, CT, L])
        dt = sb("dt", [P, 2, CT, L])
        dtu = sb("dtu", [P, CT, L])
        bcs = sb("bcs", [P, 2, L], BF16)
        xd = sb("xd", [P, L])
        t1 = sb("t1", [P, L])
        t2 = sb("t2", [P, L])
        t3 = sb("t3", [P, L])
        work = sb("work", [P, 3, CT, L])
        cbc = sb("cbc", [P, L])
        acc = sb("acc", [P, CT, L])
        x1 = sb("x1", [P, CT, L])
        xln = sb("xln", [P, CT, L])
        ring = sb("ring", [P, RING, CT * 2 * P + 2 * C])
        hid = sb("hid", [P, 2, 2, HALF])
        ytmp = sb("ytmp", [P, CT, HALF])
        gbc = sb("gbc", [P, HALF])
        small = sb("small", [P, L + C + NE * P + P])
        gt = small[0:NE, 0:L]
        b2_sb = small[0:NE, L:L + C]
        sel4 = small[0:NE, L + C:L + C + NE * P].rearrange("p (e n) -> p e n", e=NE)
        selc = small[0:NE, L + C + NE * P:]
        dtw_sb = small[3 * BC:3 * BC + R, 0:K * C].rearrange("p (k c) -> p k c", k=K)
        ident = sb("ident", [P, P])
        tri = sb("tri", [P, P])
        mean_w = sb("mean_w", [P, P])
        sel = sb("sel", [P, BC, P], BF16)
        xpw_sb = sb("xpw_sb", [P, CT, K, 3 * BC + R])
        ch = sb("ch", [P, CT, CHAN])
        nega = sb("nega", [P, CT, K * N])
        dsum = sb("dsum", [P, CT])
        b1_sb = sb("b1_sb", [P, NE * 2 * PAIRS])
        gw_sb = sb("gw_sb", [P, CT, NE])
        gb_sb = sb("gb_sb", [P, NE])
        low_sb = sb("low_sb", [P, NE, NE])
        bn = sb("bn", [P, CT, NH, 6])
        mv = sb("mv", [P, CT, 2])
        gmean = sb("gmean", [P, CT])
        gvar = sb("gvar", [P, CT])
        grstd = sb("grstd", [P, CT])
        rmax = sb("rmax", [P, 2])
        nbias = sb("nbias", [P, 2])
        rsum = sb("rsum", [P, 2])
        rinv = sb("rinv", [P, 2])
        gs = sb("gs", [P, TT, NE])
        gp = sb("gp", [P, TT, NE])
        gr = sb("gr", [P, TT])
        gi = sb("gi", [P, TT])
        cgt = sb("cgt", [P, TT, NE, NE])
        ceq = sb("ceq", [P, TT, NE, NE])
        rank = sb("rank", [P, TT, NE])
        eps_c = sb("eps_c", [P, 1])
        one_c = sb("one_c", [P, 1])

        ps = ctx.enter_context(nc.psum_tensor("ps", [P, 8 * HALF], F32))

        def banks(a, n=1):
            return ps[:, a * HALF:(a + n) * HALF]

        PB, PM, PH, PY = 0, 2, 3, 5
        BLOCKS = [(j, o) for j in range(CT) for o in range(CT) if abs(j - o) <= 1]
        gm_w = xd[:, 0:len(BLOCKS) * P].rearrange("p (g n) -> p g n", n=P)
        da, dbu, h = (work[:, i] for i in range(3))
        qt, kt = work[:, 0], work[:, 1]
        vv = work[:, 2].rearrange("p t l -> p (t l)").rearrange("p (s c) -> p s c", c=C)
        prob = [t1, t2]
        pt = t3
        wq_sb = ring[:].rearrange("p r n -> p (r n)")[:, 0:CT * 3 * C].rearrange("p (t m n) -> p t m n", t=CT, m=3)

        c_load = sem("const_loaded")
        b1_full = sem("first_biases_loaded")
        c_mem = sem("const_zeroed")
        c_pool = sem("const_built")
        c_exp = sem("const_exp")
        c_dve = sem("const_scaled")
        x_full = sem("x_loaded")
        xres_full = sem("residual_loaded")
        gn_step = sem("gn_step")
        gm_full = sem("group_blocks_loaded")
        gn_psum = sem("gn_psum")
        gn_ln = sem("gn_log")
        gn_rstd = sem("gn_rstd")
        u_ready = sem("u_normed")
        acc_init = sem("acc_started")
        misc_full = sem("misc_full")
        misc_free = sem("misc_free")
        split_step = sem("split_step")
        sp_exp = sem("softplus_exp")
        sp_ln = sem("softplus_log")
        sp_corr = sem("softplus_corrected")
        sp_one = sem("softplus_rounded")
        dt_step = sem("dt_step")
        b_full = sem("b_row_full")
        dbu_done = sem("dbu_done")
        da_done = sem("da_done")
        scan_done = sem("scan_done")
        hc_done = sem("hc_done")
        acc_done = sem("acc_done")
        ln_mean = sem("ln_mean")
        ln_cent = sem("ln_centred")
        ln_sq = sem("ln_squared")
        ln_var = sem("ln_var")
        ln_log = sem("ln_log")
        ln_rstd = sem("ln_rstd")
        ln_out = sem("ln_out")
        ssm_act = sem("ssm_activated")
        x1_ssm = sem("x1_from_scan")
        wq_full = sem("wqkv_loaded")
        qkv_full = sem("qkv_full")
        qkv_v = sem("qkv_copied_vector")
        qkv_s = sem("qkv_copied_scalar")
        s_full = sem("scores_full")
        sm_step = sem("softmax_step")
        p_exp = sem("probs_exp")
        p_norm = sem("probs_normed")
        pt_full = sem("probs_turned")
        pt_copy = sem("probs_copied")
        o_full = sem("attn_out_full")
        x1_attn = sem("x1_from_attention")
        g_full = sem("gate_scores_full")
        g_step = sem("gate_step")
        g_exp = sem("gate_exp")
        g_norm = sem("gate_normed")
        g_turn = sem("gate_turned")
        g_copy = sem("gate_copied")
        b2_full = sem("b2_full")
        b2_add = sem("b2_added")
        w_full = [sem(f"weights_loaded_{i}") for i in range(RING)]
        pair_used = sem("pair_used")
        l1_full = sem("hidden_full")
        gelu_done = sem("gelu_done")
        sel_copy = sem("expert_row_selected")
        gbc_full = sem("gate_row_full")
        gbc_copy = sem("gate_row_copied")
        y_read = sem("expert_out_read")
        x1_ffn = sem("x1_from_experts")
        out_done = sem("out_stored")

        CONST_LOADS = 7
        GN_STEPS, SPLIT_STEPS, GATE_STEPS = 13, 6, 14
        MISC_K = NH + CT * NH + 2 * N
        QKV = 2 * CT * NH + TT

        block = ctx.enter_context(nc.Block())

        def rev(ap, k):
            return ap[:, ::-1] if k >= 2 else ap

        def by_rows(ap, k):
            return ap.rearrange("p (w h) -> p h w", w=WW) if k % 2 else ap.rearrange("p (h w) -> p h w", w=WW)

        def rows(ap):
            return ap.rearrange("p (h w) -> p h w", w=WW)

        @block.sync
        def _(sp):
            for dst, src in (
                (xpw_sb[:], xpw.rearrange("(t p) k m -> p t k m", p=P)),
                (dtw_sb, dtw),
                (ch[:], chan.rearrange("(t p) m -> p t m", p=P)),
                (b2_sb, b2),
                (gw_sb[:], gate_w.rearrange("(t p) m -> p t m", p=P)),
                (gb_sb[:], gate_b), (low_sb[:], lower),
            ):
                sp.dma_start(dst, src).then_inc(c_load, 16)
            sp.dma_start(b1_sb[:], b1).then_inc(b1_full, 16)
            sp.dma_start(gm_w, gmat.rearrange("g p n -> p g n")).then_inc(gm_full, 16)
            with sp.Fori(0, NB) as b:
                sp.wait_ge(x1_ssm, b * CT + 1)
                sp.dma_start(u[:], x[bass.ds(b, 1)].rearrange("b (t p) l -> p (b t) l", p=P)).then_inc(x_full, 16)
                sp.wait_ge(dt_step, b * (9 * K) + (9 * K + 1))
                sp.dma_start(u[:], x[bass.ds(b, 1)].rearrange("b (t p) l -> p (b t) l", p=P)).then_inc(xres_full, 16)
                sp.wait_ge(pair_used, b * (NE * NH * PAIRS) + RING)
                sp.dma_start(wq_sb, wqkv.rearrange("(t p) m n -> p t m n", p=P)).then_inc(wq_full, 16)
                sp.wait_ge(qkv_full, b * QKV + QKV)
                sp.dma_start(gm_w, gmat.rearrange("g p n -> p g n")).then_inc(gm_full, 16)
                with sp.Fori(0, NE) as e:
                    for chunk in range(NH):
                        for p in range(PAIRS):
                            sp.wait_ge(pair_used, (b * NE + e) * (NH * PAIRS) + (chunk * PAIRS + p + 1))
                            sp.dma_start(ring[:, p % RING, :],
                                         wpk[bass.ds(e * PAIRS + p, 1)].rearrange("g p n -> p (g n)")
                                         ).then_inc(w_full[p % RING], 16)
                sp.wait_ge(x1_ffn, b * (NE * NH) + (NE * NH + 1))
                sp.dma_start(out[bass.ds(b, 1)].rearrange("b (t p) l -> p (b t) l", p=P), x1[:]).then_inc(out_done, 16)
            sp.wait_ge(out_done, 16 * NB + 1)
            sp.wait_ge(gm_full, 16 * (NB + 1))

        @block.gpsimd
        def _(pool):
            for t, value in ((ident[:], 0.0), (tri[:], 0.0), (sel[:], 0.0), (sel4, 0.0), (mean_w[:], 1.0 / C),
                             (eps_c[:], EPS), (one_c[:], 1.0)):
                pool.memset(t, value).then_inc(c_mem, 1)
            pool.wait_ge(c_mem, 7)
            pool.affine_select(out=ident[:], in_=ident[:], compare_op=ALU.not_equal, fill=1.0, base=0,
                               pattern=[[-1, P]], channel_multiplier=1).then_inc(c_pool, 1)
            pool.affine_select(out=tri[:], in_=tri[:], compare_op=ALU.is_ge, fill=MASKED, base=0,
                               pattern=[[-1, P]], channel_multiplier=1).then_inc(c_pool, 1)
            pool.affine_select(out=sel4, in_=sel4, compare_op=ALU.not_equal, fill=1.0, base=0,
                               pattern=[[-1, NE], [0, P]], channel_multiplier=1).then_inc(c_pool, 1)
            for part in range(3):
                pool.affine_select(out=sel[:], in_=sel[:], compare_op=ALU.not_equal, fill=1.0, base=-BC * part,
                                   pattern=[[-1, BC], [0, P]], channel_multiplier=1).then_inc(c_pool, 1)
                pool.wait_ge(c_pool, 4 + part)

            with pool.Fori(0, NB) as b:
                for k in range(K):
                    kk = b * K + k
                    for j in range(CT):
                        d = dt[:, k % 2, j, :]
                        pool.wait_ge(sp_ln, kk * CT + (j + 1))
                        pool.wait_ge(sp_corr, kk * CT + (j + 1))
                        pool.tensor_tensor(t2[:], t2[:], t3[:], ALU.add).then_inc(dt_step, 1)
                        pool.wait_ge(dt_step, kk * 9 + (3 * j + 1 + 1))
                        pool.tensor_tensor(d, d, t2[:], ALU.add).then_inc(dt_step, 1)
                        pool.wait_ge(dt_step, kk * 9 + (3 * j + 2 + 1))
                        pool.tensor_tensor(dtu[:, j, :], d, u[:, j, :], ALU.mult).then_inc(dt_step, 1)
                    with pool.Fori(0, N) as n:
                        g = kk * N + n
                        for j in range(CT):
                            if j == 0:
                                pool.wait_ge(misc_free, kk * MISC_K + n * 2 + (NH + CT * NH + 2 + 1))
                            pool.wait_ge(scan_done, g * CT + (CT + j + 1))
                            pool.tensor_tensor(h[:, j, :], h[:, j, :], cbc[:], ALU.mult).then_inc(hc_done, 1)

        @block.scalar
        def _(act):
            act.wait_ge(c_load, 16 * CONST_LOADS)
            act.wait_ge(b1_full, 16)
            act.wait_ge(c_mem, 7)
            act.activation(nega[:], ch[:, :, ALOG:ALOG + K * N], ACT.Exp).then_inc(c_exp, 1)

            def norm(c, src):
                for j in range(CT):
                    act.wait_ge(ln_cent, c * CT + (j + 1))
                    act.activation(dbu[:, j, :], src[:, j, :], ACT.Square).then_inc(ln_sq, 1)
                act.wait_ge(ln_var, c + 1)
                act.activation(t1[:], banks(PH, 2), ACT.Ln, bias=eps_c[:, 0:1]).then_inc(ln_log, 1)
                act.wait_ge(ln_log, c + 1)
                act.activation(t1[:], t1[:], ACT.Exp, scale=-0.5).then_inc(ln_rstd, 1)

            with act.Fori(0, NB) as b:
                act.wait_ge(gn_psum, b * 2 + 2)
                act.activation(gvar[:], banks(PB)[:, CT:2 * CT], ACT.Ln, bias=eps_c[:, 0:1]).then_inc(gn_ln, 1)
                act.wait_ge(gn_ln, b + 1)
                act.activation(grstd[:], gvar[:], ACT.Exp, scale=-0.5).then_inc(gn_rstd, 1)
                for k in range(K):
                    kk = b * K + k
                    m = kk * MISC_K
                    for s in range(NH):
                        if s == 0:
                            act.wait_ge(split_step, kk * SPLIT_STEPS + 1)
                        act.wait_ge(misc_full, m + (s + 1))
                        act.activation(xd[0:3 * BC + R, s * HALF:(s + 1) * HALF], banks(PM)[0:3 * BC + R, :],
                                       ACT.Copy).then_inc(misc_free, 1)
                    for j in range(CT):
                        act.wait_ge(dt_step, kk * 9 + (3 * j + 1))
                        bias = ch[:, j, DTB + k:DTB + k + 1]
                        for s in range(NH):
                            act.wait_ge(misc_full, m + (NH + j * NH + s + 1))
                            act.activation(t1[:, s * HALF:(s + 1) * HALF], banks(PM), ACT.Abs, bias=bias)
                            act.activation(dt[:, k % 2, j, s * HALF:(s + 1) * HALF], banks(PM), ACT.Relu,
                                           bias=bias).then_inc(misc_free, 1)
                        act.wait_ge(misc_free, m + (NH + j * NH + 2 + 1))
                        act.activation(t1[:], t1[:], ACT.Exp, scale=-1.0).then_inc(sp_exp, 1)
                        act.wait_ge(sp_exp, kk * CT + (j + 1))
                        act.activation(t2[:], t1[:], ACT.Ln, bias=one_c[:, 0:1]).then_inc(sp_ln, 1)
                    act.wait_ge(dt_step, kk * 9 + 10)
                    with act.Fori(0, N) as n:
                        g = kk * N + n
                        for j in range(CT):
                            act.wait_ge(scan_done, g * CT + (j + 1))
                            act.wait_ge(c_dve, 2)
                            act.activation(by_rows(da[:, j, :], k), rows(dt[:, k % 2, j, :]), ACT.Exp,
                                           scale=nega[:, j, bass.ds(n + k * N, 1)]).then_inc(da_done, 1)
                            if j == 0:
                                for s in range(NH):
                                    if s == 0:
                                        act.wait_ge(hc_done, g * CT + 1)
                                    act.wait_ge(misc_full, m + n * 2 + (NH + CT * NH + s + 1))
                                    act.activation(by_rows(cbc[:], k)[:, s * (HH // NH):(s + 1) * (HH // NH), :],
                                                   rows(banks(PM)), ACT.Copy).then_inc(misc_free, 1)
                norm(b * 3, acc)
                for j in range(CT):
                    act.wait_ge(ln_out, b * (3 * CT) + (j + 1))
                    act.activation(dbu[:, j, :], acc[:, j, :], ACT.Gelu, scale=ch[:, j, LNW:LNW + 1],
                                   bias=ch[:, j, LNB:LNB + 1]).then_inc(ssm_act, 1)
                norm(b * 3 + 1, xln)
                for i in range(1, QKV, 2):
                    act.wait_ge(qkv_full, b * QKV + (i + 1))
                    if i < 2 * CT * NH:
                        dst = (qt, kt)[i // (CT * NH)][:, i // NH % CT, (i % NH) * HALF:(i % NH + 1) * HALF]
                        src = banks(i % 8)
                    else:
                        dst, src = vv[:, i - 2 * CT * NH, :], banks(i % 8)[:, 0:C]
                    act.activation(dst, src, ACT.Copy).then_inc(qkv_s, 1)

                def turned(i):
                    w = (i + 1) * P
                    act.wait_ge(pt_full, b * TT + (i + 1))
                    if i >= 1:
                        act.wait_ge(o_full, b * TT + i)
                    act.activation(pt[:, 0:w], banks(4, 2)[:, 0:w], ACT.Copy).then_inc(pt_copy, 1)

                for i in range(TT):
                    w = (i + 1) * P
                    act.wait_ge(sm_step, b * (3 * TT) + 3 * (i + 1))
                    if i >= 2:
                        act.wait_ge(pt_full, b * TT + (i - 1))
                    act.activation(prob[i % 2][:, 0:w], banks(2 * (i % 2), 2)[:, 0:w], ACT.Exp, scale=SCALE,
                                   bias=nbias[:, i % 2:i % 2 + 1], accum_out=rsum[:, i % 2:i % 2 + 1]).then_inc(p_exp, 1)
                    if i >= 1:
                        turned(i - 1)
                turned(TT - 1)
                norm(b * 3 + 2, xln)
                act.wait_ge(g_step, b * GATE_STEPS + 3)
                act.activation(gp[:], gs[:], ACT.Exp).then_inc(g_exp, 1)
                act.wait_ge(g_turn, b + 1)
                act.activation(gt, banks(PY, 2)[0:NE, :], ACT.Copy).then_inc(g_copy, 1)
                for e in range(NE):
                    act.activation(selc, sel4[:, e, :],
                                   ACT.Copy).then_inc(sel_copy, 1)
                    for chunk in range(NH):
                        ec = (b * NE + e) * NH + chunk
                        for p in range(PAIRS):
                            for s in range(2):
                                if s == 0:
                                    act.wait_ge(pair_used, ec * PAIRS + (p + RING - 1))
                                act.wait_ge(l1_full, ec * (2 * PAIRS) + (2 * p + s + 1))
                                act.activation(hid[:, p % 2, s, :], banks(PH + s), ACT.Gelu,
                                               bias=b1_sb[:, (e * PAIRS + p) * 2 + s:(e * PAIRS + p) * 2 + s + 1]
                                               ).then_inc(gelu_done, 1)
                            if p == 0:
                                act.wait_ge(gbc_full, ec + 1)
                                act.activation(gbc[:], banks(PY), ACT.Copy).then_inc(gbc_copy, 1)

        @block.vector
        def _(dve):
            for s in (x1_ssm, split_step, dt_step, misc_free, hc_done, gelu_done, dbu_done, y_read, x1_ffn, out_done):
                dve.sem_inc(s, 1)
            dve.sem_inc(scan_done, CT)
            dve.sem_inc(acc_done, CT)
            dve.sem_inc(pair_used, RING)
            dve.wait_ge(c_exp, 1)
            dve.tensor_scalar(nega[:], nega[:], -1.0, None, ALU.mult).then_inc(c_dve, 1)
            dve.tensor_reduce(dsum[:], ch[:, :, DSK:DSK + K], AX.X, ALU.add).then_inc(c_dve, 1)
            dve.wait_ge(c_dve, 2)

            def norm(c, src, dst):
                dve.wait_ge(ln_mean, c + 1)
                for j in range(CT):
                    dve.tensor_tensor(dst[:, j, :], src[:, j, :], banks(PB, 2), ALU.subtract).then_inc(ln_cent, 1)
                dve.wait_ge(ln_rstd, c + 1)
                for j in range(CT):
                    dve.tensor_tensor(dst[:, j, :], dst[:, j, :], t1[:], ALU.mult).then_inc(ln_out, 1)

            with dve.Fori(0, NB) as b:
                dve.wait_ge(x_full, b * 16 + 16)
                for j in range(CT):
                    for s in range(NH):
                        dve.bn_stats(bn[:, j, s, :], u[:, j, s * HALF:(s + 1) * HALF]).then_inc(gn_step, 1)
                g0 = b * GN_STEPS
                dve.wait_ge(gn_step, g0 + 6)
                dve.memset(gmean[:], 0.0)
                for j in range(CT):
                    dve.bn_aggr(mv[:, j, :], bn[:, j, :, :]).then_inc(gn_step, 1)
                dve.wait_ge(gn_psum, b * 2 + 1)
                dve.tensor_copy(gmean[:], banks(PB)[:, 0:CT]).then_inc(gn_step, 1)
                dve.wait_ge(gn_step, g0 + 10)
                dve.tensor_tensor(gvar[:], mv[:, :, 0], gmean[:], ALU.subtract).then_inc(gn_step, 1)
                dve.wait_ge(gn_step, g0 + 11)
                dve.tensor_tensor(gvar[:], gvar[:], gvar[:], ALU.mult).then_inc(gn_step, 1)
                dve.wait_ge(gn_step, g0 + 12)
                dve.tensor_tensor(mv[:, :, 1], mv[:, :, 1], gvar[:], ALU.add).then_inc(gn_step, 1)
                dve.wait_ge(gn_rstd, b + 1)
                for j in range(CT):
                    dve.tensor_scalar(u[:, j, :], u[:, j, :], gmean[:, j:j + 1], grstd[:, j:j + 1],
                                      ALU.subtract, ALU.mult).then_inc(u_ready, 1)
                for j in range(CT):
                    dve.wait_ge(u_ready, b * CT + (j + 1))
                    dve.tensor_scalar(acc[:, j, :], u[:, j, :], dsum[:, j:j + 1], None, ALU.mult).then_inc(acc_init, 1)
                for k in range(K):
                    kk = b * K + k
                    s0 = kk * SPLIT_STEPS
                    S, rows3 = bcs[:, k % 2, :], 3 * BC
                    dve.wait_ge(misc_free, kk * MISC_K + (NH + 1))
                    dve.tensor_copy(S[0:rows3], xd[0:rows3]).then_inc(split_step, 1)
                    dve.wait_ge(split_step, s0 + 2)
                    dve.tensor_tensor(t3[0:rows3], xd[0:rows3], S[0:rows3], ALU.subtract).then_inc(split_step, 1)
                    dve.wait_ge(split_step, s0 + 3)
                    dve.tensor_copy(S[BC:2 * BC], t3[BC:2 * BC]).then_inc(split_step, 1)
                    dve.tensor_copy(S[2 * BC:rows3], t3[2 * BC:rows3]).then_inc(split_step, 1)
                    dve.wait_ge(split_step, s0 + 5)
                    dve.tensor_tensor(t3[2 * BC:rows3], t3[2 * BC:rows3], S[2 * BC:rows3], ALU.subtract).then_inc(split_step, 1)
                    dve.wait_ge(split_step, s0 + 6)
                    dve.tensor_copy(S[2 * BC:rows3], t3[2 * BC:rows3]).then_inc(split_step, 1)
                    dve.wait_ge(split_step, s0 + 7)
                    for j in range(CT):
                        dve.wait_ge(sp_exp, kk * CT + (j + 1))
                        dve.wait_ge(dt_step, kk * 9 + (3 * j + 1))
                        dve.tensor_scalar(t3[:], t1[:], 1.0, -1.0, ALU.add, ALU.add).then_inc(sp_one, 1)
                        dve.wait_ge(sp_one, kk * CT + (j + 1))
                        dve.tensor_tensor(t3[:], t1[:], t3[:], ALU.subtract).then_inc(sp_corr, 1)

                    def inputs(g, first=False):
                        for j in range(CT):
                            if j == 0:
                                if first:
                                    dve.wait_ge(dt_step, kk * 9 + 10)
                                dve.wait_ge(b_full, g + 1)
                            dve.wait_ge(scan_done, g * CT + (j + 1))
                            dve.tensor_tensor(by_rows(dbu[:, j, :], k), rows(dtu[:, j, :]), rows(banks(PB, 2)),
                                              ALU.mult).then_inc(dbu_done, 1)

                    def scans(g):
                        for j in range(CT):
                            dve.wait_ge(da_done, g * CT + (j + 1))
                            dve.wait_ge(dbu_done, g * CT + (j + 1 + 1))
                            dve.wait_ge(acc_done, g * CT + (j + 1))
                            dve.tensor_tensor_scan(rev(h[:, j, :], k), rev(da[:, j, :], k), rev(dbu[:, j, :], k),
                                                   0.0, ALU.mult, ALU.add).then_inc(scan_done, 1)

                    def sums(g):
                        for j in range(CT):
                            dve.wait_ge(hc_done, g * CT + (j + 1 + 1))
                            dve.tensor_tensor(rows(acc[:, j, :]), rows(acc[:, j, :]), by_rows(h[:, j, :], k),
                                              ALU.add).then_inc(acc_done, 1)

                    inputs(kk * N, True)
                    with dve.Fori(0, N - 1) as n:
                        g = kk * N + n
                        scans(g)
                        inputs(g + 1)
                        sums(g)
                    scans(kk * N + (N - 1))
                    sums(kk * N + (N - 1))

                norm(b * 3, acc, acc)
                dve.wait_ge(xres_full, b * 16 + 16)
                for j in range(CT):
                    dve.wait_ge(ssm_act, b * CT + (j + 1))
                    if j == 0:
                        dve.wait_ge(out_done, b * 16 + 1)
                    dve.tensor_tensor(x1[:, j, :], dbu[:, j, :], u[:, j, :], ALU.add).then_inc(x1_ssm, 1)
                norm(b * 3 + 1, x1, xln)
                for i in range(0, QKV, 2):
                    dve.wait_ge(qkv_full, b * QKV + (i + 1))
                    if i < 2 * CT * NH:
                        dst = (qt, kt)[i // (CT * NH)][:, i // NH % CT, (i % NH) * HALF:(i % NH + 1) * HALF]
                        src = banks(i % 8)
                    else:
                        dst, src = vv[:, i - 2 * CT * NH, :], banks(i % 8)[:, 0:C]
                    dve.tensor_copy(dst, src).then_inc(qkv_v, 1)

                def maximum(i):
                    w, s0, r = (i + 1) * P, b * (3 * TT), i % 2
                    sc = banks(2 * r, 2)
                    dve.wait_ge(s_full, b * TT + (i + 1))
                    dve.tensor_tensor(sc[:, i * P:w], sc[:, i * P:w], tri[:], ALU.add).then_inc(sm_step, 1)
                    dve.wait_ge(sm_step, s0 + (3 * i + 1))
                    dve.tensor_reduce(rmax[:, r:r + 1], sc[:, 0:w], AX.X, ALU.max).then_inc(sm_step, 1)
                    dve.wait_ge(sm_step, s0 + (3 * i + 2))
                    dve.tensor_scalar(nbias[:, r:r + 1], rmax[:, r:r + 1], -SCALE, None, ALU.mult).then_inc(sm_step, 1)

                def weights(i):
                    w, r = (i + 1) * P, i % 2
                    dve.wait_ge(p_exp, b * TT + (i + 1))
                    dve.reciprocal(rinv[:, r:r + 1], rsum[:, r:r + 1]).then_inc(p_norm, 1)
                    dve.wait_ge(p_norm, b * (2 * TT) + (2 * i + 1))
                    dve.tensor_scalar(prob[r][:, 0:w], prob[r][:, 0:w], rinv[:, r:r + 1], None, ALU.mult).then_inc(p_norm, 1)

                def attended(i):
                    dve.wait_ge(o_full, b * TT + (i + 1))
                    t = x1[:, :, i * P:(i + 1) * P]
                    dve.tensor_tensor(t, t, banks(6 + i % 2)[:, 0:C].rearrange("p (t n) -> p t n", t=CT),
                                      ALU.add).then_inc(x1_attn, 1)

                maximum(0)
                for i in range(TT):
                    if i + 1 < TT:
                        maximum(i + 1)
                    weights(i)
                    if i >= 1:
                        attended(i - 1)
                attended(TT - 1)
                norm(b * 3 + 2, x1, xln)
                g0 = b * GATE_STEPS
                count = [0]

                def step(ins):
                    count[0] += 1
                    ins.then_inc(g_step, 1)
                    dve.wait_ge(g_step, g0 + count[0])

                def each(ap):
                    return ap.unsqueeze(2).broadcast_to([P, TT, NE])

                dve.wait_ge(g_full, b + 1)
                step(dve.tensor_tensor(gs[:], banks(PM)[:, 0:TT * NE].rearrange("p (t e) -> p t e", e=NE),
                                       gb_sb[:].unsqueeze(1).broadcast_to([P, TT, NE]), ALU.add))
                step(dve.tensor_reduce(gr[:], gs[:], AX.X, ALU.max))
                step(dve.tensor_tensor(gs[:], gs[:], each(gr[:]), ALU.subtract))
                dve.wait_ge(g_exp, b + 1)
                step(dve.tensor_reduce(gr[:], gp[:], AX.X, ALU.add))
                step(dve.reciprocal(gi[:], gr[:]))
                step(dve.tensor_tensor(gp[:], gp[:], each(gi[:]), ALU.mult))
                other = gp[:].unsqueeze(2).broadcast_to([P, TT, NE, NE])
                own = gp[:].unsqueeze(3).broadcast_to([P, TT, NE, NE])
                step(dve.tensor_tensor(cgt[:], other, own, ALU.is_gt))
                step(dve.tensor_tensor(ceq[:], other, own, ALU.is_equal))
                step(dve.tensor_tensor(ceq[:], ceq[:], low_sb[:].unsqueeze(1).broadcast_to([P, TT, NE, NE]), ALU.mult))
                step(dve.tensor_tensor(cgt[:], cgt[:], ceq[:], ALU.add))
                step(dve.tensor_reduce(rank[:], cgt[:], AX.X, ALU.add))
                step(dve.scalar_tensor_tensor(out=gp[:], in0=rank[:], scalar=1.5, in1=gp[:], op0=ALU.is_lt, op1=ALU.mult))
                step(dve.tensor_reduce(gr[:], gp[:], AX.X, ALU.add))
                dve.tensor_scalar(gr[:], gr[:], 1e-9, None, ALU.add).then_inc(g_step, 1)
                assert count[0] + 1 == GATE_STEPS, count
                dve.wait_ge(g_step, g0 + GATE_STEPS)
                dve.reciprocal(gi[:], gr[:]).then_inc(g_norm, 1)
                dve.wait_ge(g_norm, b * 2 + 1)
                dve.tensor_tensor(gp[:], gp[:], each(gi[:]), ALU.mult).then_inc(g_norm, 1)
                for i in range(CT * NH):
                    dve.wait_ge(b2_full, b * (CT * NH) + (i + 1))
                    t = x1[:, i // NH, (i % NH) * HALF:(i % NH + 1) * HALF]
                    dve.tensor_tensor(t, t, banks((0, 1, 3, 4, 5, 6)[i]), ALU.add).then_inc(b2_add, 1)
                with dve.Fori(0, NE) as e:
                    for chunk in range(NH):
                        ec = (b * NE + e) * NH + chunk
                        dve.wait_ge(pair_used, ec * PAIRS + (PAIRS + RING))
                        dve.wait_ge(gbc_copy, ec + 1)
                        dve.wait_ge(x1_ffn, ec + 1)
                        dve.tensor_tensor(ytmp[:], banks(PY, CT).rearrange("p (t n) -> p t n", t=CT),
                                          gbc[:].unsqueeze(1).broadcast_to([P, CT, HALF]), ALU.mult).then_inc(y_read, 1)
                        dve.wait_ge(y_read, ec + 2)
                        t = x1[:, :, chunk * HALF:(chunk + 1) * HALF]
                        dve.tensor_tensor(t, t, ytmp[:], ALU.add).then_inc(x1_ffn, 1)

        @block.tensor
        def _(pe):
            pe.wait_ge(c_load, 16 * CONST_LOADS)
            pe.wait_ge(c_pool, 6)

            def norm(c, src):
                for s in range(NH):
                    for j in range(CT):
                        mm = pe.matmul(banks(PB + s), mean_w[:], src[:, j, s * HALF:(s + 1) * HALF],
                                       start=(j == 0), stop=(j == CT - 1))
                mm.then_inc(ln_mean, 1)
                pe.wait_ge(ln_sq, c * CT + CT)
                for s in range(NH):
                    for j in range(CT):
                        mm = pe.matmul(banks(PH + s), mean_w[:], dbu[:, j, s * HALF:(s + 1) * HALF],
                                       start=(j == 0), stop=(j == CT - 1))
                mm.then_inc(ln_var, 1)

            with pe.Fori(0, NB) as b:
                pe.wait_ge(gm_full, b * 16 + 16)
                for stat in range(2):
                    pe.wait_ge(gn_step, b * GN_STEPS + (9, 13)[stat])
                    for o in range(CT):
                        near = [j for j in range(CT) if (j, o) in BLOCKS]
                        for j in near:
                            mm = pe.matmul(banks(PB)[:, stat * CT + o:stat * CT + o + 1], gm_w[:, BLOCKS.index((j, o)), :],
                                           mv[:, j, stat:stat + 1], start=(j == near[0]), stop=(j == near[-1]))
                    mm.then_inc(gn_psum, 1)
                for k in range(K):
                    kk = b * K + k
                    m = kk * MISC_K
                    if k == 0:
                        pe.wait_ge(u_ready, b * CT + CT)
                    for s in range(NH):
                        pe.wait_ge(misc_free, m + s + 1)
                        for j in range(CT):
                            mm = pe.matmul(banks(PM)[0:3 * BC + R, :], xpw_sb[:, j, k, :],
                                           u[:, j, s * HALF:(s + 1) * HALF], start=(j == 0), stop=(j == CT - 1))
                        mm.then_inc(misc_full, 1)
                    for i in range(CT * NH):
                        j, s = i // NH, i % NH
                        pe.wait_ge(misc_free, m + (NH + i + 1))
                        pe.matmul(banks(PM), dtw_sb[:, k, j * P:(j + 1) * P],
                                  xd[3 * BC:3 * BC + R, s * HALF:(s + 1) * HALF], start=True, stop=True
                                  ).then_inc(misc_full, 1)
                    S = bcs[0:3 * BC, k % 2, :]
                    with pe.Fori(0, N) as n:
                        pe.wait_ge(split_step, kk * SPLIT_STEPS + (SPLIT_STEPS + 1))
                        pe.wait_ge(dbu_done, (kk * N + n) * CT + 1)
                        for s in range(NH):
                            mm = pe.matmul(banks(PB + s), sel[0:3 * BC, bass.ds(n, 1), :].rearrange("p a n -> p (a n)"),
                                           S[:, s * HALF:(s + 1) * HALF], start=True, stop=True)
                        mm.then_inc(b_full, 1)
                        for s in range(NH):
                            pe.wait_ge(misc_free, m + n * 2 + (NH + CT * NH + s + 1))
                            pe.matmul(banks(PM), sel[0:3 * BC, bass.ds(n + N, 1), :].rearrange("p a n -> p (a n)"),
                                      S[:, s * HALF:(s + 1) * HALF], start=True, stop=True).then_inc(misc_full, 1)
                pe.wait_ge(acc_done, b * (K * N * CT) + (K * N * CT + CT))
                norm(b * 3, acc)
                pe.wait_ge(x1_ssm, b * CT + (CT + 1))
                norm(b * 3 + 1, x1)
                pe.wait_ge(wq_full, b * 16 + 16)
                pe.wait_ge(ln_out, b * (3 * CT) + 2 * CT)
                for i in range(QKV):
                    if i >= 8:
                        pe.wait_ge((qkv_v, qkv_s)[i % 2], b * (QKV // 2) + ((i - 8) // 2 + 1))
                    for c in range(CT):
                        if i < 2 * CT * NH:
                            which, o, s = i // (CT * NH), i // NH % CT, i % NH
                            mm = pe.matmul(banks(i % 8), wq_sb[:, c, which, o * P:(o + 1) * P],
                                           xln[:, c, s * HALF:(s + 1) * HALF], start=(c == 0), stop=(c == CT - 1))
                        else:
                            s = i - 2 * CT * NH
                            mm = pe.matmul(banks(i % 8)[:, 0:C], xln[:, c, s * P:(s + 1) * P],
                                           wq_sb[:, c, 2, :], start=(c == 0), stop=(c == CT - 1))
                    mm.then_inc(qkv_full, 1)
                pe.wait_ge(qkv_v, b * (QKV // 2) + QKV // 2)
                pe.wait_ge(qkv_s, b * (QKV // 2) + QKV // 2)

                def scores(i):
                    w = (i + 1) * P
                    if i >= 2:
                        pe.wait_ge(p_exp, b * TT + (i - 1))
                    for a in range(0, w, HALF):
                        z = min(w, a + HALF)
                        for c in range(CT):
                            mm = pe.matmul(banks(2 * (i % 2), 2)[:, a:z], qt[:, c, i * P:(i + 1) * P], kt[:, c, a:z],
                                           start=(c == 0), stop=(c == CT - 1))
                    mm.then_inc(s_full, 1)

                scores(0)
                for i in range(TT):
                    if i + 1 < TT:
                        scores(i + 1)
                    pe.wait_ge(p_norm, b * (2 * TT) + (2 * i + 2))
                    if i >= 1:
                        pe.wait_ge(pt_copy, b * TT + i)
                    for s in range(i + 1):
                        mm = pe.transpose(banks(4, 2)[:, s * P:(s + 1) * P], prob[i % 2][:, s * P:(s + 1) * P], ident[:])
                    mm.then_inc(pt_full, 1)
                    pe.wait_ge(pt_copy, b * TT + (i + 1))
                    if i >= 2:
                        pe.wait_ge(x1_attn, b * TT + (i - 1))
                    for o in range(CT):
                        for s in range(i + 1):
                            mm = pe.matmul(banks(6 + i % 2)[:, o * P:(o + 1) * P], vv[:, s, o * P:(o + 1) * P],
                                           pt[:, s * P:(s + 1) * P], start=(s == 0), stop=(s == i))
                    mm.then_inc(o_full, 1)
                pe.wait_ge(x1_attn, b * TT + TT)
                norm(b * 3 + 2, x1)
                pe.wait_ge(ln_out, b * (3 * CT) + 3 * CT)
                for t in range(TT):
                    for c in range(CT):
                        mm = pe.matmul(banks(PM)[:, t * NE:(t + 1) * NE], xln[:, c, t * P:(t + 1) * P], gw_sb[:, c, :],
                                       start=(c == 0), stop=(c == CT - 1))
                mm.then_inc(g_full, 1)
                pe.wait_ge(g_norm, b * 2 + 2)
                for t in range(TT):
                    mm = pe.transpose(banks(PY, 2)[0:NE, t * P:(t + 1) * P], gp[:, t, :], ident[:])
                mm.then_inc(g_turn, 1)
                pe.wait_ge(g_copy, b + 1)
                for i in range(CT * NH):
                    pe.matmul(banks((0, 1, 3, 4, 5, 6)[i]), b2_sb[:, i // NH * P:(i // NH + 1) * P],
                              gt[:, (i % NH) * HALF:(i % NH + 1) * HALF], start=True, stop=True).then_inc(b2_full, 1)
                with pe.Fori(0, NE) as e:
                    for chunk in range(NH):
                        ec = (b * NE + e) * NH + chunk
                        cols = slice(chunk * HALF, (chunk + 1) * HALF)

                        def first(p):
                            w1 = ring[:, p % RING, 0:CT * 2 * P].rearrange("p (t n) -> p t n", t=CT)
                            pe.wait_ge(w_full[p % RING], ec * (16 * PAIRS // RING) + 16 * (p // RING + 1))
                            pe.wait_ge(gelu_done, ec * (2 * PAIRS) + (2 * p + 1))
                            for s in range(2):
                                for c in range(CT):
                                    mm = pe.matmul(banks(PH + s), w1[:, c, s * P:(s + 1) * P], xln[:, c, cols],
                                                   start=(c == 0), stop=(c == CT - 1))
                                mm.then_inc(l1_full, 1)

                        def second(p):
                            w2 = ring[:, p % RING, CT * 2 * P:].rearrange("p (t n) -> p t n", t=2)
                            if p == 0:
                                pe.wait_ge(gbc_copy, ec + 1)
                            pe.wait_ge(gelu_done, ec * (2 * PAIRS) + (2 * p + 2 + 1))
                            for o in range(CT):
                                for s in range(2):
                                    mm = pe.matmul(banks(PY + o), w2[:, s, o * P:(o + 1) * P], hid[:, p % 2, s, :],
                                                   start=(p == 0 and s == 0), stop=(p == PAIRS - 1 and s == 1))
                            mm.then_inc(pair_used, 1)

                        if chunk == 0:
                            pe.wait_ge(b2_add, b * (CT * NH) + CT * NH)
                        first(0)
                        pe.wait_ge(y_read, ec + 1)
                        if chunk == 0:
                            pe.wait_ge(sel_copy, b * NE + e + 1)
                        pe.matmul(banks(PY), selc, gt[:, cols], start=True, stop=True).then_inc(gbc_full, 1)
                        for p in range(1, PAIRS):
                            first(p)
                            second(p - 1)
                        second(PAIRS - 1)


_INS = ["x", "xpw", "dtw", "chan", "wqkv", "gate_w", "gate_b", "b1", "b2", "wpk", "gmat", "lower"]


def kernel(**inputs):
    import numpy as np
    import concourse.bacc as bacc
    from concourse.bass_utils import run_bass_kernel_spmd

    a = {k: np.ascontiguousarray(v) for k, v in inputs.items()}
    proj = a["L0_conv_x_proj_weight"].transpose(2, 0, 1)
    rows = proj[:, :, R:]
    per_channel = [a["L0_conv_dt_projs_bias"].T,
                   a["L0_conv_A_logs"].reshape(K, C, N).transpose(1, 0, 2).reshape(C, K * N),
                   a["L0_conv_Ds"].reshape(K, C).T, a["L0_conv_ln_weight"][:, None], a["L0_conv_ln_bias"][:, None]]
    w1 = a["L1_ffn_w1"].reshape(NE, CT, P, PAIRS, 2 * P).transpose(0, 3, 2, 1, 4).reshape(NE * PAIRS, P, CT * 2 * P)
    w2 = a["L1_ffn_w2"].reshape(NE, PAIRS, 2, P, C).transpose(0, 1, 3, 2, 4).reshape(NE * PAIRS, P, 2 * C)
    groups = np.arange(C) // GROUP
    gmat = (groups[:, None] == groups[None]).astype(np.float32) / np.float32(GROUP)
    data = {
        "x": a["x"].reshape(NB, C, L),
        "xpw": np.concatenate([rows, rows, rows, proj[:, :, :R]], axis=2),
        "dtw": a["L0_conv_dt_projs_weight"].transpose(2, 0, 1),
        "chan": np.concatenate(per_channel, axis=1),
        "wqkv": np.stack([a["L1_attn_Wq"], a["L1_attn_Wk"], a["L1_attn_Wv"]], axis=1),
        "gate_w": a["L1_ffn_gate_w"],
        "gate_b": np.repeat(a["L1_ffn_gate_b"][None], P, axis=0),
        "b1": a["L1_ffn_b1"].reshape(NE, 2 * PAIRS, P).transpose(2, 0, 1).reshape(P, NE * 2 * PAIRS),
        "b2": a["L1_ffn_b2"],
        "wpk": np.concatenate([w1, w2], axis=2),
        "gmat": np.stack([gmat[j * P:(j + 1) * P, o * P:(o + 1) * P]
                          for j in range(CT) for o in range(CT) if abs(j - o) <= 1]),
        "lower": np.repeat(np.tril(np.ones((NE, NE), np.float32), -1)[None], P, axis=0),
    }
    nc = bacc.Bacc("TRN2", target_bir_lowering=False, num_devices=1)
    arrays, aps = {}, []
    for name in _INS:
        arr = np.ascontiguousarray(data[name])
        arrays[f"in_{name}"] = arr
        aps.append(nc.dram_tensor(f"in_{name}", arr.shape, mybir.dt.from_np(arr.dtype), kind="ExternalInput").ap())
    out = nc.dram_tensor("out_0", (NB, C, L), F32, kind="ExternalOutput").ap()
    build(nc, *aps, out)
    r = run_bass_kernel_spmd(nc, [arrays], core_ids=[0])
    return r.results[0]["out_0"].reshape(NB, C, HH, WW)
```

```python
from contextlib import ExitStack

import concourse.bass as bass
from concourse import mybir

F32 = mybir.dt.float32
BF16 = mybir.dt.bfloat16
ALU = mybir.AluOpType
ACT = mybir.ActivationFunctionType
AX = mybir.AxisListType

P = 128
NB, C, HH, WW = 4, 384, 32, 32
L = HH * WW
CT = C // P
HALF = 512
NH = L // HALF
K, N, R = 4, 16, 12
BC = 2 * N
TT = L // P
NE, HID = 4, 4 * C
PAIRS = HID // (2 * P)
GROUP = C // 32
EPS = 1e-5
MASKED = -1e30
RING = 3
SCALE = float(C) ** -0.5
DTB, ALOG, DSK, LNW, LNB, CHAN = 0, K, K + K * N, 2 * K + K * N, 2 * K + K * N + 1, 2 * K + K * N + 2


def build(nc, x, xpw, dtw, chan, wqkv, gate_w, gate_b, b1, b2, wpk, gmat, lower, out):
    with ExitStack() as ctx:
        def sb(name, shape, dt=F32):
            return ctx.enter_context(nc.sbuf_tensor(name, shape, dt))

        def sem(name):
            return ctx.enter_context(nc.semaphore(name))

        u = sb("u", [P, CT, L])
        dt = sb("dt", [P, CT, L])
        spare = sb("spare", [P, CT, L])
        dtu = sb("dtu", [P, CT, L])
        bcs = sb("bcs", [P, 2, L], BF16)
        xd = sb("xd", [P, L])
        tmp = sb("tmp", [P, CT, L])
        work = sb("work", [P, 3, CT, L])
        cbc = sb("cbc", [P, 2, L])
        acc = sb("acc", [P, CT, L])
        x1 = sb("x1", [P, CT, L])
        xln = sb("xln", [P, CT, L])
        ring = sb("ring", [P, RING, CT * 2 * P + 2 * C])
        hid = sb("hid", [P, 2, 2, HALF])
        qt = sb("qt", [P, CT, P])
        ytmp = sb("ytmp", [P, CT, HALF])
        gbc = sb("gbc", [P, HALF])
        small = sb("small", [P, L + C + NE * P + P])
        gt = small[0:NE, 0:L]
        b2_sb = small[0:NE, L:L + C]
        sel4 = small[0:NE, L + C:L + C + NE * P].rearrange("p (e n) -> p e n", e=NE)
        selc = small[0:NE, L + C + NE * P:]
        dtw_sb = small[3 * BC:3 * BC + R, 0:K * C].rearrange("p (k c) -> p k c", k=K)
        ident = sb("ident", [P, P])
        tri = sb("tri", [P, P])
        mean_w = sb("mean_w", [P, P])
        sel = sb("sel", [P, BC, P], BF16)
        xpw_sb = sb("xpw_sb", [P, CT, K, 3 * BC + R])
        ch = sb("ch", [P, CT, CHAN])
        nega = ch[:, :, ALOG:ALOG + K * N]
        dsum = sb("dsum", [P, CT])
        b1_sb = sb("b1_sb", [P, NE * 2 * PAIRS])
        gw_sb = sb("gw_sb", [P, CT, NE])
        gb_sb = sb("gb_sb", [P, NE])
        low_sb = sb("low_sb", [P, NE, NE])
        bn = sb("bn", [P, CT, NH, 6])
        mv = sb("mv", [P, CT, 2])
        gmean = sb("gmean", [P, CT])
        gvar = sb("gvar", [P, CT])
        grstd = sb("grstd", [P, CT])
        rmax = sb("rmax", [P, 2])
        nbias = sb("nbias", [P, 2])
        rsum = sb("rsum", [P, 2])
        rinv = sb("rinv", [P, 2])
        eps_c = sb("eps_c", [P, 1])
        one_c = sb("one_c", [P, 1])

        ps = ctx.enter_context(nc.psum_tensor("ps", [P, 8 * HALF], F32))

        def banks(a, n=1):
            return ps[:, a * HALF:(a + n) * HALF]

        PB, PM, PH, PY = 0, 2, 3, 5
        PO = 7
        BLOCKS = [(j, o) for j in range(CT) for o in range(CT) if abs(j - o) <= 1]
        gm_w = xd[:, 0:len(BLOCKS) * P].rearrange("p (g n) -> p g n", n=P)
        da, dbu, h = (work[:, i] for i in range(3))
        t1, t2, t3 = (tmp[:, i, :] for i in range(3))
        kt = tmp
        vv = spare[:].rearrange("p t l -> p (t l)").rearrange("p (s c) -> p s c", c=C)
        prob = [hid[:, i].rearrange("p s n -> p (s n)") for i in range(2)]
        gs, gp, rank = (spare[:, 0, i * TT * NE:(i + 1) * TT * NE].rearrange("p (t e) -> p t e", e=NE) for i in range(3))
        gr, gi = (spare[:, 0, (12 + i) * TT:(13 + i) * TT] for i in range(2))
        cgt, ceq = (spare[:, 1, i * TT * NE * NE:(i + 1) * TT * NE * NE].rearrange("p (t e f) -> p t e f", e=NE, f=NE)
                    for i in range(2))
        rstd = prob[0]
        pt = ytmp[:].rearrange("p t n -> p (t n)")[:, 0:L]
        wq_sb = ring[:].rearrange("p r n -> p (r n)")[:, 0:CT * 3 * C].rearrange("p (t m n) -> p t m n", t=CT, m=3)

        c_load = sem("const_loaded")
        b1_full = sem("first_biases_loaded")
        c_mem = sem("const_zeroed")
        c_pool = sem("const_built")
        c_exp = sem("const_exp")
        c_dve = sem("const_scaled")
        x_full = sem("x_loaded")
        xres_full = sem("residual_loaded")
        gn_step = sem("gn_step")
        gm_full = sem("group_blocks_loaded")
        gn_psum = sem("gn_psum")
        gn_ln = sem("gn_log")
        gn_rstd = sem("gn_rstd")
        u_ready = sem("u_normed")
        acc_init = sem("acc_started")
        misc_full = sem("misc_full")
        misc_free = sem("misc_free")
        split_step = sem("split_step")
        sp_exp = sem("softplus_exp")
        sp_ln = sem("softplus_log")
        sp_corr = sem("softplus_corrected")
        sp_one = sem("softplus_rounded")
        dt_step = sem("dt_step")
        b_full = sem("b_row_full")
        dbu_done = sem("dbu_done")
        da_done = sem("da_done")
        scan_done = sem("scan_done")
        hc_done = sem("hc_done")
        acc_done = sem("acc_done")
        ln_mean = sem("ln_mean")
        ln_cent = sem("ln_centred")
        ln_sq = sem("ln_squared")
        ln_var = sem("ln_var")
        ln_log = sem("ln_log")
        ln_rstd = sem("ln_rstd")
        ln_out = sem("ln_out")
        ssm_act = sem("ssm_activated")
        x1_ssm = sem("x1_from_scan")
        wq_full = sem("wqkv_loaded")
        kv_full = sem("kv_full")
        kv_copy = sem("kv_copied")
        q_full = sem("q_full")
        q_copy = sem("q_copied")
        s_full = sem("scores_full")
        sm_step = sem("softmax_step")
        p_exp = sem("probs_exp")
        p_norm = sem("probs_normed")
        pt_full = sem("probs_turned")
        pt_copy = sem("probs_copied")
        o_full = sem("attn_out_full")
        x1_attn = sem("x1_from_attention")
        g_full = sem("gate_scores_full")
        g_step = sem("gate_step")
        g_exp = sem("gate_exp")
        g_norm = sem("gate_normed")
        g_turn = sem("gate_turned")
        g_copy = sem("gate_copied")
        b2_load = sem("second_biases_loaded")
        b2_full = sem("b2_full")
        b2_add = sem("b2_added")
        w_full = [sem(f"weights_loaded_{i}") for i in range(RING)]
        pair_used = sem("pair_used")
        l1_full = sem("hidden_full")
        gelu_done = sem("gelu_done")
        sel_copy = sem("expert_row_selected")
        gbc_full = sem("gate_row_full")
        gbc_copy = sem("gate_row_copied")
        y_read = sem("expert_out_read")
        x1_ffn = sem("x1_from_experts")
        out_done = sem("out_stored")

        CONST_LOADS = 6
        GN_STEPS, SPLIT_STEPS, GATE_STEPS = 13, 6, 14
        MISC_K = NH + CT * NH + 2 * N
        KV = TT + CT * NH
        E_B = NE * NH
        PAIRS_B = E_B * PAIRS

        block = ctx.enter_context(nc.Block())

        def rev(ap, k):
            return ap[:, ::-1] if k >= 2 else ap

        def by_rows(ap, k):
            return ap.rearrange("p (w h) -> p h w", w=WW) if k % 2 else ap.rearrange("p (h w) -> p h w", w=WW)

        def rows(ap):
            return ap.rearrange("p (h w) -> p h w", w=WW)


        @block.sync
        def _(sp):
            for dst, src in (
                (xpw_sb[:], xpw.rearrange("(t p) k m -> p t k m", p=P)),
                (dtw_sb, dtw),
                (ch[:], chan.rearrange("(t p) m -> p t m", p=P)),
                (gw_sb[:], gate_w.rearrange("(t p) m -> p t m", p=P)),
                (gb_sb[:], gate_b), (low_sb[:], lower),
            ):
                sp.dma_start(dst, src).then_inc(c_load, 16)
            sp.dma_start(b1_sb[:], b1).then_inc(b1_full, 16)

            def image(b):
                return x[bass.ds(b, 1)].rearrange("b (t p) l -> p (b t) l", p=P)

            def experts(b, e0, e1):
                with sp.Fori(e0, e1) as e:
                    for chunk in range(NH):
                        for p in range(PAIRS):
                            sp.wait_ge(pair_used, (b * NE + e) * (NH * PAIRS) + (chunk * PAIRS + p + 1))
                            sp.dma_start(ring[:, p % RING, :],
                                         wpk[bass.ds(e * PAIRS + p, 1)].rearrange("g p n -> p (g n)")
                                         ).then_inc(w_full[p % RING], 16)

            def attention_weights(b):
                sp.wait_ge(pair_used, b * PAIRS_B + RING)
                sp.dma_start(wq_sb, wqkv.rearrange("(t p) m n -> p t m n", p=P)).then_inc(wq_full, 16)

            def residual(b):
                sp.wait_ge(dt_step, b * (9 * K) + (9 * K + 1))
                sp.dma_start(u[:], image(b)).then_inc(xres_full, 16)

            def store(b):
                sp.wait_ge(x1_ffn, b * E_B + (E_B + 1))
                sp.dma_start(out[bass.ds(b, 1)].rearrange("b (t p) l -> p (b t) l", p=P), x1[:]).then_inc(out_done, 16)

            sp.dma_start(gm_w, gmat.rearrange("g p n -> p g n")).then_inc(gm_full, 16)
            sp.dma_start(u[:], image(0)).then_inc(x_full, 16)
            residual(0)
            with sp.Fori(1, NB) as b:
                attention_weights(b - 1)
                sp.wait_ge(x1_ssm, b * CT + 1)
                sp.dma_start(gm_w, gmat.rearrange("g p n -> p g n")).then_inc(gm_full, 16)
                sp.dma_start(u[:], image(b)).then_inc(x_full, 16)
                sp.wait_ge(q_full, (b - 1) * TT + TT)
                sp.dma_start(b2_sb, b2).then_inc(b2_load, 16)
                experts(b - 1, 0, NE - 1)
                residual(b)
                experts(b - 1, NE - 1, NE)
                store(b - 1)
            attention_weights(NB - 1)
            sp.wait_ge(q_full, NB * TT)
            sp.dma_start(b2_sb, b2).then_inc(b2_load, 16)
            experts(NB - 1, 0, NE)
            store(NB - 1)
            sp.wait_ge(out_done, 16 * NB + 1)

        @block.gpsimd
        def _(pool):
            for t, value in ((ident[:], 0.0), (tri[:], 0.0), (sel[:], 0.0), (sel4, 0.0), (mean_w[:], 1.0 / C),
                             (eps_c[:], EPS), (one_c[:], 1.0)):
                pool.memset(t, value).then_inc(c_mem, 1)
            pool.wait_ge(c_mem, 7)
            pool.affine_select(out=ident[:], in_=ident[:], compare_op=ALU.not_equal, fill=1.0, base=0,
                               pattern=[[-1, P]], channel_multiplier=1).then_inc(c_pool, 1)
            pool.affine_select(out=tri[:], in_=tri[:], compare_op=ALU.is_ge, fill=MASKED, base=0,
                               pattern=[[-1, P]], channel_multiplier=1).then_inc(c_pool, 1)
            pool.affine_select(out=sel4, in_=sel4, compare_op=ALU.not_equal, fill=1.0, base=0,
                               pattern=[[-1, NE], [0, P]], channel_multiplier=1).then_inc(c_pool, 1)
            for part in range(3):
                pool.affine_select(out=sel[:], in_=sel[:], compare_op=ALU.not_equal, fill=1.0, base=-BC * part,
                                   pattern=[[-1, BC], [0, P]], channel_multiplier=1).then_inc(c_pool, 1)
                pool.wait_ge(c_pool, 4 + part)

            with pool.Fori(0, NB) as b:
                for k in range(K):
                    kk = b * K + k
                    for j in range(CT):
                        d = dt[:, j, :]
                        pool.wait_ge(sp_ln, kk * CT + (j + 1))
                        pool.wait_ge(sp_corr, kk * CT + (j + 1))
                        pool.tensor_tensor(t2, t2, t3, ALU.add).then_inc(dt_step, 1)
                        pool.wait_ge(dt_step, kk * 9 + (3 * j + 2))
                        pool.tensor_tensor(d, d, t2, ALU.add).then_inc(dt_step, 1)
                        pool.wait_ge(dt_step, kk * 9 + (3 * j + 3))
                        pool.tensor_tensor(dtu[:, j, :], d, u[:, j, :], ALU.mult).then_inc(dt_step, 1)
                    with pool.Fori(0, N, 2) as n:
                        for odd in range(2):
                            for j in range(CT):
                                if j == 0:
                                    pool.wait_ge(misc_free, kk * MISC_K + n * 2 + (2 * odd + NH + CT * NH + 3))
                                pool.wait_ge(scan_done, (kk * N + n) * CT + (odd * CT + CT + j + 1))
                                pool.tensor_tensor(h[:, j, :], h[:, j, :], cbc[:, odd, :], ALU.mult).then_inc(hc_done, 1)

        @block.scalar
        def _(act):
            act.wait_ge(c_load, 16 * CONST_LOADS)
            act.wait_ge(b1_full, 16)
            act.wait_ge(c_mem, 7)
            act.activation(nega, ch[:, :, ALOG:ALOG + K * N], ACT.Exp).then_inc(c_exp, 1)

            def norm_squares(c, src, sq):
                for j in range(CT):
                    act.wait_ge(ln_cent, c * CT + (j + 1))
                    act.activation(sq[:, j, :], src[:, j, :], ACT.Square).then_inc(ln_sq, 1)

            def norm_rstd(c, r):
                act.wait_ge(ln_var, c + 1)
                act.activation(r, banks(PH, 2), ACT.Ln, bias=eps_c[:, 0:1]).then_inc(ln_log, 1)
                act.wait_ge(ln_log, c + 1)
                act.activation(r, r, ACT.Exp, scale=-0.5).then_inc(ln_rstd, 1)

            def group_norm(b):
                act.wait_ge(gn_psum, b * 2 + 2)
                act.activation(gvar[:], banks(PB)[:, CT:2 * CT], ACT.Ln, bias=eps_c[:, 0:1]).then_inc(gn_ln, 1)
                act.wait_ge(gn_ln, b + 1)
                act.activation(grstd[:], gvar[:], ACT.Exp, scale=-0.5).then_inc(gn_rstd, 1)

            def prepare(b, k):
                kk = b * K + k
                m = kk * MISC_K
                for s in range(NH):
                    if s == 0:
                        act.wait_ge(split_step, kk * SPLIT_STEPS + 1)
                    act.wait_ge(misc_full, m + (s + 1))
                    act.activation(xd[0:3 * BC + R, s * HALF:(s + 1) * HALF], banks(PM)[0:3 * BC + R, :],
                                   ACT.Copy).then_inc(misc_free, 1)
                for j in range(CT):
                    act.wait_ge(dt_step, kk * 9 + (3 * j + 1))
                    bias = ch[:, j, DTB + k:DTB + k + 1]
                    for s in range(NH):
                        act.wait_ge(misc_full, m + (NH + j * NH + s + 1))
                        act.activation(t1[:, s * HALF:(s + 1) * HALF], banks(PM), ACT.Abs, bias=bias)
                        act.activation(dt[:, j, s * HALF:(s + 1) * HALF], banks(PM), ACT.Relu,
                                       bias=bias).then_inc(misc_free, 1)
                    act.wait_ge(misc_free, m + (NH + j * NH + 3))
                    act.activation(t1, t1, ACT.Exp, scale=-1.0).then_inc(sp_exp, 1)
                    act.wait_ge(sp_exp, kk * CT + (j + 1))
                    act.activation(t2, t1, ACT.Ln, bias=one_c[:, 0:1]).then_inc(sp_ln, 1)
                act.wait_ge(dt_step, kk * 9 + 10)

            def decay(b, k, n, j):
                act.wait_ge(scan_done, ((b * K + k) * N + n) * CT + (j + 1))
                act.wait_ge(c_dve, 2)
                act.activation(by_rows(da[:, j, :], k), rows(dt[:, j, :]), ACT.Exp,
                               scale=nega[:, j, bass.ds(n + k * N, 1)]).then_inc(da_done, 1)

            def c_half(b, k, n, par, s):
                kk = b * K + k
                if s == 0:
                    act.wait_ge(hc_done, (kk * N + n - 1) * CT + 1)
                act.wait_ge(misc_full, kk * MISC_K + n * 2 + (NH + CT * NH + s + 1))
                act.activation(by_rows(cbc[:, par, :], k)[:, s * (HH // NH):(s + 1) * (HH // NH), :],
                               rows(banks(PM)), ACT.Copy).then_inc(misc_free, 1)

            def first_row(b, k):
                kk = b * K + k
                for s in range(NH):
                    if s == 0:
                        act.wait_ge(hc_done, kk * N * CT + 1)
                    act.wait_ge(misc_full, kk * MISC_K + (NH + CT * NH + s + 1))
                    act.activation(by_rows(cbc[:, 0, :], k)[:, s * (HH // NH):(s + 1) * (HH // NH), :],
                                   rows(banks(PM)), ACT.Copy).then_inc(misc_free, 1)

            def state(b, k, n, par, last=False):
                decay(b, k, n, 0)
                if not last:
                    c_half(b, k, n + 1, 1 - par, 0)
                decay(b, k, n, 1)
                if not last:
                    c_half(b, k, n + 1, 1 - par, 1)
                decay(b, k, n, 2)

            def scan_back(b):
                norm_squares(b * 3, acc, dbu)
                norm_rstd(b * 3, t1)
                for j in range(CT):
                    act.wait_ge(ln_out, b * (3 * CT) + (j + 1))
                    act.activation(dbu[:, j, :], acc[:, j, :], ACT.Gelu, scale=ch[:, j, LNW:LNW + 1],
                                   bias=ch[:, j, LNB:LNB + 1]).then_inc(ssm_act, 1)

            def kv_copies(b, i0, i1):
                for i in range(i0, i1):
                    act.wait_ge(kv_full, b * KV + (i + 1))
                    src = banks(PH + i % 2)
                    if i < TT:
                        act.activation(vv[:, i, :], src[:, 0:C], ACT.Copy).then_inc(kv_copy, 1)
                    else:
                        o, s = (i - TT) // NH, (i - TT) % NH
                        act.activation(kt[:, o, s * HALF:(s + 1) * HALF], src, ACT.Copy).then_inc(kv_copy, 1)

            def q_tile(b, i):
                act.wait_ge(q_full, b * TT + (i + 1))
                act.activation(qt[:], banks(PO)[:, 0:C].rearrange("p (t n) -> p t n", t=CT), ACT.Copy).then_inc(q_copy, 1)

            def probs(b, i):
                w = (i + 1) * P
                act.wait_ge(sm_step, b * (3 * TT) + 3 * (i + 1))
                if i >= 2:
                    act.wait_ge(pt_full, b * TT + (i - 1))
                act.activation(prob[i % 2][:, 0:w], banks(PY, 2)[:, 0:w], ACT.Exp, scale=SCALE,
                               bias=nbias[:, i % 2:i % 2 + 1], accum_out=rsum[:, i % 2:i % 2 + 1]).then_inc(p_exp, 1)

            def turned(b, i):
                w = (i + 1) * P
                act.wait_ge(pt_full, b * TT + (i + 1))
                if i >= 1:
                    act.wait_ge(o_full, b * TT + i)
                act.activation(pt[:, 0:w], banks(PH, 2)[:, 0:w], ACT.Copy).then_inc(pt_copy, 1)

            def gate_exp(b):
                act.wait_ge(g_step, b * GATE_STEPS + 3)
                act.activation(gp, gs, ACT.Exp).then_inc(g_exp, 1)

            def gate_rows(b):
                act.wait_ge(g_turn, b + 1)
                act.activation(gt, banks(PY, 2)[0:NE, :], ACT.Copy).then_inc(g_copy, 1)

            def gate_row(b, ec):
                act.wait_ge(gbc_full, b * E_B + (ec + 1))
                act.activation(gbc[:], banks(PY), ACT.Copy).then_inc(gbc_copy, 1)

            def activate(b, q):
                e, chunk, p = q // (NH * PAIRS), q // PAIRS % NH, q % PAIRS
                if p == 0 and chunk == 0:
                    act.activation(selc, sel4[:, e, :], ACT.Copy).then_inc(sel_copy, 1)
                if p == 1:
                    gate_row(b, q // PAIRS)
                act.wait_ge(pair_used, b * PAIRS_B + (q + RING - 1))
                for s in range(2):
                    col = 2 * (e * PAIRS + p) + s
                    act.wait_ge(l1_full, b * (2 * PAIRS_B) + (2 * q + s + 1))
                    act.activation(hid[:, p % 2, s, :], banks(PH + s), ACT.Gelu,
                                   bias=b1_sb[:, col:col + 1]).then_inc(gelu_done, 1)

            def attention_slot(b, n):
                if n < 2:
                    kv_copies(b, TT + n * CT, TT + (n + 1) * CT)
                i = n - 2
                if 0 <= i < TT:
                    q_tile(b, i)
                if 1 <= i <= TT:
                    turned(b, i - 1)
                if 0 <= i < TT:
                    probs(b, i)
                if n == 11:
                    norm_squares(b * 3 + 2, xln, spare)
                if n == 12:
                    norm_rstd(b * 3 + 2, rstd)
                if n == 13:
                    gate_exp(b)
                if n == 14:
                    gate_rows(b)

            def attention_start(b):
                norm_squares(b * 3 + 1, xln, tmp)
                norm_rstd(b * 3 + 1, rstd)
                kv_copies(b, 0, TT)

            group_norm(0)
            for k in range(K):
                prepare(0, k)
                first_row(0, k)
                with act.Fori(0, N - 2, 2) as n:
                    state(0, k, n, 0)
                    state(0, k, n + 1, 1)
                state(0, k, N - 2, 0)
                state(0, k, N - 1, 1, True)
            scan_back(0)
            with act.Fori(1, NB) as b:
                attention_start(b - 1)
                group_norm(b)
                for k in range(K):
                    prepare(b, k)
                    first_row(b, k)
                    for n in range(N):
                        state(b, k, n, n % 2, n == N - 1)
                        if k == 0:
                            attention_slot(b - 1, n)
                        else:
                            activate(b - 1, (k - 1) * N + n)
                scan_back(b)
            attention_start(NB - 1)
            for n in range(N):
                attention_slot(NB - 1, n)
            for q in range(PAIRS_B):
                activate(NB - 1, q)

        @block.vector
        def _(dve):
            for s in (x1_ssm, split_step, dt_step, misc_free, hc_done, gelu_done, dbu_done, y_read, x1_ffn, out_done):
                dve.sem_inc(s, 1)
            dve.sem_inc(scan_done, CT)
            dve.sem_inc(acc_done, CT)
            dve.sem_inc(pair_used, RING)
            dve.wait_ge(c_exp, 1)
            dve.tensor_scalar(nega, nega, -1.0, None, ALU.mult).then_inc(c_dve, 1)
            dve.tensor_reduce(dsum[:], ch[:, :, DSK:DSK + K], AX.X, ALU.add).then_inc(c_dve, 1)
            dve.wait_ge(c_dve, 2)

            def norm_centre(c, src, dst, bank):
                dve.wait_ge(ln_mean, c + 1)
                for j in range(CT):
                    dve.tensor_tensor(dst[:, j, :], src[:, j, :], banks(bank, 2), ALU.subtract).then_inc(ln_cent, 1)

            def norm_scale(c, dst, r):
                dve.wait_ge(ln_rstd, c + 1)
                for j in range(CT):
                    dve.tensor_tensor(dst[:, j, :], dst[:, j, :], r, ALU.mult).then_inc(ln_out, 1)

            def group_norm(b):
                g0 = b * GN_STEPS
                dve.wait_ge(x_full, b * 16 + 16)
                for j in range(CT):
                    for s in range(NH):
                        dve.bn_stats(bn[:, j, s, :], u[:, j, s * HALF:(s + 1) * HALF]).then_inc(gn_step, 1)
                dve.wait_ge(gn_step, g0 + 6)
                dve.memset(gmean[:], 0.0)
                for j in range(CT):
                    dve.bn_aggr(mv[:, j, :], bn[:, j, :, :]).then_inc(gn_step, 1)
                dve.wait_ge(gn_psum, b * 2 + 1)
                dve.tensor_copy(gmean[:], banks(PB)[:, 0:CT]).then_inc(gn_step, 1)
                dve.wait_ge(gn_step, g0 + 10)
                dve.tensor_tensor(gvar[:], mv[:, :, 0], gmean[:], ALU.subtract).then_inc(gn_step, 1)
                dve.wait_ge(gn_step, g0 + 11)
                dve.tensor_tensor(gvar[:], gvar[:], gvar[:], ALU.mult).then_inc(gn_step, 1)
                dve.wait_ge(gn_step, g0 + 12)
                dve.tensor_tensor(mv[:, :, 1], mv[:, :, 1], gvar[:], ALU.add).then_inc(gn_step, 1)
                dve.wait_ge(gn_rstd, b + 1)
                for j in range(CT):
                    dve.tensor_scalar(u[:, j, :], u[:, j, :], gmean[:, j:j + 1], grstd[:, j:j + 1],
                                      ALU.subtract, ALU.mult).then_inc(u_ready, 1)
                for j in range(CT):
                    dve.wait_ge(u_ready, b * CT + (j + 1))
                    dve.tensor_scalar(acc[:, j, :], u[:, j, :], dsum[:, j:j + 1], None, ALU.mult).then_inc(acc_init, 1)

            def prepare(b, k):
                kk = b * K + k
                s0 = kk * SPLIT_STEPS
                S, rows3 = bcs[:, k % 2, :], 3 * BC
                dve.wait_ge(misc_free, kk * MISC_K + (NH + 1))
                dve.tensor_copy(S[0:rows3], xd[0:rows3]).then_inc(split_step, 1)
                dve.wait_ge(split_step, s0 + 2)
                dve.tensor_tensor(t3[0:rows3], xd[0:rows3], S[0:rows3], ALU.subtract).then_inc(split_step, 1)
                dve.wait_ge(split_step, s0 + 3)
                dve.tensor_copy(S[BC:2 * BC], t3[BC:2 * BC]).then_inc(split_step, 1)
                dve.tensor_copy(S[2 * BC:rows3], t3[2 * BC:rows3]).then_inc(split_step, 1)
                dve.wait_ge(split_step, s0 + 5)
                dve.tensor_tensor(t3[2 * BC:rows3], t3[2 * BC:rows3], S[2 * BC:rows3], ALU.subtract).then_inc(split_step, 1)
                dve.wait_ge(split_step, s0 + 6)
                dve.tensor_copy(S[2 * BC:rows3], t3[2 * BC:rows3]).then_inc(split_step, 1)
                dve.wait_ge(split_step, s0 + 7)
                for j in range(CT):
                    dve.wait_ge(sp_exp, kk * CT + (j + 1))
                    dve.wait_ge(dt_step, kk * 9 + (3 * j + 1))
                    dve.tensor_scalar(t3, t1, 1.0, -1.0, ALU.add, ALU.add).then_inc(sp_one, 1)
                    dve.wait_ge(sp_one, kk * CT + (j + 1))
                    dve.tensor_tensor(t3, t1, t3, ALU.subtract).then_inc(sp_corr, 1)

            def inputs(b, k, n, first=False):
                g = (b * K + k) * N + n
                for j in range(CT):
                    if j == 0:
                        if first:
                            dve.wait_ge(dt_step, (b * K + k) * 9 + 10)
                        dve.wait_ge(b_full, g + 1)
                    dve.wait_ge(scan_done, g * CT + (j + 1))
                    dve.tensor_tensor(by_rows(dbu[:, j, :], k), rows(dtu[:, j, :]), rows(banks(PB, 2)),
                                      ALU.mult).then_inc(dbu_done, 1)

            def scans(b, k, n):
                g = (b * K + k) * N + n
                for j in range(CT):
                    dve.wait_ge(da_done, g * CT + (j + 1))
                    dve.wait_ge(dbu_done, g * CT + (j + 2))
                    dve.wait_ge(acc_done, g * CT + (j + 1))
                    dve.tensor_tensor_scan(rev(h[:, j, :], k), rev(da[:, j, :], k), rev(dbu[:, j, :], k),
                                           0.0, ALU.mult, ALU.add).then_inc(scan_done, 1)

            def sums(b, k, n):
                g = (b * K + k) * N + n
                for j in range(CT):
                    dve.wait_ge(hc_done, g * CT + (j + 2))
                    dve.tensor_tensor(rows(acc[:, j, :]), rows(acc[:, j, :]), by_rows(h[:, j, :], k),
                                      ALU.add).then_inc(acc_done, 1)

            def scan_back(b):
                norm_centre(b * 3, acc, acc, PB)
                norm_scale(b * 3, acc, t1)
                dve.wait_ge(xres_full, b * 16 + 16)
                for j in range(CT):
                    dve.wait_ge(ssm_act, b * CT + (j + 1))
                    if j == 0:
                        dve.wait_ge(out_done, b * 16 + 1)
                    dve.tensor_tensor(x1[:, j, :], dbu[:, j, :], u[:, j, :], ALU.add).then_inc(x1_ssm, 1)

            def maximum(b, i):
                w, s0, r = (i + 1) * P, b * (3 * TT), i % 2
                sc = banks(PY, 2)
                dve.wait_ge(s_full, b * TT + (i + 1))
                dve.tensor_tensor(sc[:, i * P:w], sc[:, i * P:w], tri[:], ALU.add).then_inc(sm_step, 1)
                dve.wait_ge(sm_step, s0 + (3 * i + 1))
                dve.tensor_reduce(rmax[:, r:r + 1], sc[:, 0:w], AX.X, ALU.max).then_inc(sm_step, 1)
                dve.wait_ge(sm_step, s0 + (3 * i + 2))
                dve.tensor_scalar(nbias[:, r:r + 1], rmax[:, r:r + 1], -SCALE, None, ALU.mult).then_inc(sm_step, 1)

            def weights(b, i):
                w, r = (i + 1) * P, i % 2
                dve.wait_ge(p_exp, b * TT + (i + 1))
                dve.reciprocal(rinv[:, r:r + 1], rsum[:, r:r + 1]).then_inc(p_norm, 1)
                dve.wait_ge(p_norm, b * (2 * TT) + (2 * i + 1))
                dve.tensor_scalar(prob[r][:, 0:w], prob[r][:, 0:w], rinv[:, r:r + 1], None, ALU.mult).then_inc(p_norm, 1)

            def attended(b, i):
                dve.wait_ge(o_full, b * TT + (i + 1))
                t = x1[:, :, i * P:(i + 1) * P]
                dve.tensor_tensor(t, t, banks(PO)[:, 0:C].rearrange("p (t n) -> p t n", t=CT),
                                  ALU.add).then_inc(x1_attn, 1)

            def each(ap):
                return ap.unsqueeze(2).broadcast_to([P, TT, NE])

            def gate(b):
                g0 = b * GATE_STEPS
                count = [0]

                def step(ins):
                    count[0] += 1
                    ins.then_inc(g_step, 1)
                    dve.wait_ge(g_step, g0 + count[0])

                dve.wait_ge(g_full, b + 1)
                step(dve.tensor_tensor(gs, banks(PO)[:, 0:TT * NE].rearrange("p (t e) -> p t e", e=NE),
                                       gb_sb[:].unsqueeze(1).broadcast_to([P, TT, NE]), ALU.add))
                step(dve.tensor_reduce(gr, gs, AX.X, ALU.max))
                step(dve.tensor_tensor(gs, gs, each(gr), ALU.subtract))
                dve.wait_ge(g_exp, b + 1)
                step(dve.tensor_reduce(gr, gp, AX.X, ALU.add))
                step(dve.reciprocal(gi, gr))
                step(dve.tensor_tensor(gp, gp, each(gi), ALU.mult))
                other = gp.unsqueeze(2).broadcast_to([P, TT, NE, NE])
                own = gp.unsqueeze(3).broadcast_to([P, TT, NE, NE])
                step(dve.tensor_tensor(cgt, other, own, ALU.is_gt))
                step(dve.tensor_tensor(ceq, other, own, ALU.is_equal))
                step(dve.tensor_tensor(ceq, ceq, low_sb[:].unsqueeze(1).broadcast_to([P, TT, NE, NE]), ALU.mult))
                step(dve.tensor_tensor(cgt, cgt, ceq, ALU.add))
                step(dve.tensor_reduce(rank, cgt, AX.X, ALU.add))
                step(dve.scalar_tensor_tensor(out=gp, in0=rank, scalar=1.5, in1=gp, op0=ALU.is_lt, op1=ALU.mult))
                step(dve.tensor_reduce(gr, gp, AX.X, ALU.add))
                step(dve.tensor_scalar(gr, gr, 1e-9, None, ALU.add))
                assert count[0] == GATE_STEPS, count
                dve.reciprocal(gi, gr).then_inc(g_norm, 1)
                dve.wait_ge(g_norm, b * 2 + 1)
                dve.tensor_tensor(gp, gp, each(gi), ALU.mult).then_inc(g_norm, 1)

            def second_biases(b):
                for i in range(CT * NH):
                    dve.wait_ge(b2_full, b * (CT * NH) + (i + 1))
                    t = x1[:, i // NH, (i % NH) * HALF:(i % NH + 1) * HALF]
                    dve.tensor_tensor(t, t, banks(PH + i % 5), ALU.add).then_inc(b2_add, 1)

            def expert_out(b, ec):
                g = b * E_B + ec
                dve.wait_ge(pair_used, g * PAIRS + (PAIRS + RING))
                dve.wait_ge(gbc_copy, g + 1)
                dve.wait_ge(x1_ffn, g + 1)
                dve.tensor_tensor(ytmp[:], banks(PY, CT).rearrange("p (t n) -> p t n", t=CT),
                                  gbc[:].unsqueeze(1).broadcast_to([P, CT, HALF]), ALU.mult).then_inc(y_read, 1)
                dve.wait_ge(y_read, g + 2)
                chunk = ec % NH
                t = x1[:, :, chunk * HALF:(chunk + 1) * HALF]
                dve.tensor_tensor(t, t, ytmp[:], ALU.add).then_inc(x1_ffn, 1)

            def attention_slot(b, n, part):
                i = n - 2
                if part == 0:
                    if 0 <= i < TT:
                        maximum(b, i)
                    if n == 11:
                        norm_centre(b * 3 + 2, x1, xln, PY)
                    if n == 13:
                        norm_scale(b * 3 + 2, xln, rstd)
                    if n == 15:
                        second_biases(b)
                if part == 1 and 0 <= i < TT:
                    weights(b, i)
                if part == 2:
                    if 1 <= i <= TT:
                        attended(b, i - 1)
                    if n == 13:
                        gate(b)

            def attention_start(b):
                norm_centre(b * 3 + 1, x1, xln, PY)
                norm_scale(b * 3 + 1, xln, rstd)

            group_norm(0)
            for k in range(K):
                prepare(0, k)
                inputs(0, k, 0, True)
                with dve.Fori(0, N - 1) as n:
                    scans(0, k, n)
                    inputs(0, k, n + 1)
                    sums(0, k, n)
                scans(0, k, N - 1)
                sums(0, k, N - 1)
            scan_back(0)
            with dve.Fori(1, NB) as b:
                attention_start(b - 1)
                group_norm(b)
                for k in range(K):
                    prepare(b, k)
                    inputs(b, k, 0, True)
                    for n in range(N):
                        scans(b, k, n)
                        if k == 0:
                            attention_slot(b - 1, n, 0)
                        if n + 1 < N:
                            inputs(b, k, n + 1)
                        if k == 0:
                            attention_slot(b - 1, n, 1)
                        sums(b, k, n)
                        if k == 0:
                            attention_slot(b - 1, n, 2)
                        elif ((k - 1) * N + n) % PAIRS == 0 and (k, n) != (1, 0):
                            expert_out(b - 1, ((k - 1) * N + n) // PAIRS - 1)
                expert_out(b - 1, E_B - 1)
                scan_back(b)
            attention_start(NB - 1)
            for n in range(N):
                for part in range(3):
                    attention_slot(NB - 1, n, part)
            for ec in range(E_B):
                expert_out(NB - 1, ec)

        @block.tensor
        def _(pe):
            pe.wait_ge(c_load, 16 * CONST_LOADS)
            pe.wait_ge(c_pool, 6)

            def over_channels(bank, src):
                for s in range(NH):
                    for j in range(CT):
                        mm = pe.matmul(banks(bank + s), mean_w[:], src[:, j, s * HALF:(s + 1) * HALF],
                                       start=(j == 0), stop=(j == CT - 1))
                return mm

            def norm_mean(bank, src):
                over_channels(bank, src).then_inc(ln_mean, 1)

            def norm_var(c, sq):
                pe.wait_ge(ln_sq, c * CT + CT)
                over_channels(PH, sq).then_inc(ln_var, 1)

            def group_norm(b):
                pe.wait_ge(gm_full, b * 16 + 16)
                for stat in range(2):
                    pe.wait_ge(gn_step, b * GN_STEPS + (9, 13)[stat])
                    for o in range(CT):
                        near = [j for j in range(CT) if (j, o) in BLOCKS]
                        for j in near:
                            mm = pe.matmul(banks(PB)[:, stat * CT + o:stat * CT + o + 1], gm_w[:, BLOCKS.index((j, o)), :],
                                           mv[:, j, stat:stat + 1], start=(j == near[0]), stop=(j == near[-1]))
                    mm.then_inc(gn_psum, 1)

            def prepare(b, k):
                m = (b * K + k) * MISC_K
                if k == 0:
                    pe.wait_ge(u_ready, b * CT + CT)
                for s in range(NH):
                    pe.wait_ge(misc_free, m + (s + 1))
                    for j in range(CT):
                        mm = pe.matmul(banks(PM)[0:3 * BC + R, :], xpw_sb[:, j, k, :],
                                       u[:, j, s * HALF:(s + 1) * HALF], start=(j == 0), stop=(j == CT - 1))
                    mm.then_inc(misc_full, 1)
                for i in range(CT * NH):
                    j, s = i // NH, i % NH
                    pe.wait_ge(misc_free, m + (NH + i + 1))
                    pe.matmul(banks(PM), dtw_sb[:, k, j * P:(j + 1) * P],
                              xd[3 * BC:3 * BC + R, s * HALF:(s + 1) * HALF], start=True, stop=True
                              ).then_inc(misc_full, 1)

            def b_row(b, k, n):
                kk = b * K + k
                S = bcs[0:3 * BC, k % 2, :]
                pe.wait_ge(split_step, kk * SPLIT_STEPS + (SPLIT_STEPS + 1))
                pe.wait_ge(dbu_done, (kk * N + n) * CT + 1)
                for s in range(NH):
                    mm = pe.matmul(banks(PB + s), sel[0:3 * BC, bass.ds(n, 1), :].rearrange("p a n -> p (a n)"),
                                   S[:, s * HALF:(s + 1) * HALF], start=True, stop=True)
                mm.then_inc(b_full, 1)

            def c_half(b, k, n, s):
                kk = b * K + k
                pe.wait_ge(misc_free, kk * MISC_K + n * 2 + (NH + CT * NH + s + 1))
                pe.matmul(banks(PM), sel[0:3 * BC, bass.ds(n + N, 1), :].rearrange("p a n -> p (a n)"),
                          bcs[0:3 * BC, k % 2, s * HALF:(s + 1) * HALF], start=True, stop=True).then_inc(misc_full, 1)

            def state_rows(b, k, n):
                b_row(b, k, n)
                c_half(b, k, n, 0)
                c_half(b, k, n, 1)

            def scan_back(b):
                pe.wait_ge(acc_done, b * (K * N * CT) + (K * N * CT + CT))
                norm_mean(PB, acc)
                norm_var(b * 3, dbu)

            def kv_groups(b, i0, i1):
                for i in range(i0, i1):
                    if i >= 2:
                        pe.wait_ge(kv_copy, b * KV + (i - 1))
                    for c in range(CT):
                        if i < TT:
                            mm = pe.matmul(banks(PH + i % 2)[:, 0:C], xln[:, c, i * P:(i + 1) * P],
                                           wq_sb[:, c, 2, :], start=(c == 0), stop=(c == CT - 1))
                        else:
                            o, s = (i - TT) // NH, (i - TT) % NH
                            mm = pe.matmul(banks(PH + i % 2), wq_sb[:, c, 1, o * P:(o + 1) * P],
                                           xln[:, c, s * HALF:(s + 1) * HALF], start=(c == 0), stop=(c == CT - 1))
                    mm.then_inc(kv_full, 1)

            def q_tile(b, i):
                if i >= 2:
                    pe.wait_ge(x1_attn, b * TT + (i - 1))
                for o in range(CT):
                    for c in range(CT):
                        mm = pe.matmul(banks(PO)[:, o * P:(o + 1) * P], wq_sb[:, c, 0, o * P:(o + 1) * P],
                                       xln[:, c, i * P:(i + 1) * P], start=(c == 0), stop=(c == CT - 1))
                mm.then_inc(q_full, 1)

            def scores(b, i):
                w = (i + 1) * P
                if i == 0:
                    pe.wait_ge(kv_copy, b * KV + KV)
                else:
                    pe.wait_ge(p_exp, b * TT + i)
                pe.wait_ge(q_copy, b * TT + (i + 1))
                for a in range(0, w, HALF):
                    z = min(w, a + HALF)
                    for c in range(CT):
                        mm = pe.matmul(banks(PY, 2)[:, a:z], qt[:, c, :], kt[:, c, a:z],
                                       start=(c == 0), stop=(c == CT - 1))
                mm.then_inc(s_full, 1)

            def turn(b, i):
                pe.wait_ge(p_norm, b * (2 * TT) + (2 * i + 2))
                for s in range(i + 1):
                    mm = pe.transpose(banks(PH, 2)[:, s * P:(s + 1) * P], prob[i % 2][:, s * P:(s + 1) * P], ident[:])
                mm.then_inc(pt_full, 1)

            def attend(b, i):
                if i >= 1:
                    pe.wait_ge(x1_attn, b * TT + i)
                pe.wait_ge(pt_copy, b * TT + (i + 1))
                for o in range(CT):
                    for s in range(i + 1):
                        mm = pe.matmul(banks(PO)[:, o * P:(o + 1) * P], vv[:, s, o * P:(o + 1) * P],
                                       pt[:, s * P:(s + 1) * P], start=(s == 0), stop=(s == i))
                mm.then_inc(o_full, 1)

            def gate_scores(b):
                pe.wait_ge(ln_out, b * (3 * CT) + 3 * CT)
                for t in range(TT):
                    for c in range(CT):
                        mm = pe.matmul(banks(PO)[:, t * NE:(t + 1) * NE], xln[:, c, t * P:(t + 1) * P], gw_sb[:, c, :],
                                       start=(c == 0), stop=(c == CT - 1))
                mm.then_inc(g_full, 1)

            def gate_turn(b):
                pe.wait_ge(g_norm, b * 2 + 2)
                for t in range(TT):
                    mm = pe.transpose(banks(PY, 2)[0:NE, t * P:(t + 1) * P], gp[:, t, :], ident[:])
                mm.then_inc(g_turn, 1)

            def second_biases(b):
                pe.wait_ge(g_copy, b + 1)
                pe.wait_ge(b2_load, b * 16 + 16)
                for i in range(CT * NH):
                    if i == 5:
                        pe.wait_ge(b2_add, b * (CT * NH) + 1)
                    pe.matmul(banks(PH + i % 5), b2_sb[:, i // NH * P:(i // NH + 1) * P],
                              gt[:, (i % NH) * HALF:(i % NH + 1) * HALF], start=True, stop=True).then_inc(b2_full, 1)

            def attention_start(b):
                pe.wait_ge(x1_ssm, b * CT + (CT + 1))
                norm_mean(PY, x1)
                norm_var(b * 3 + 1, tmp)
                pe.wait_ge(wq_full, b * 16 + 16)
                pe.wait_ge(ln_out, b * (3 * CT) + 2 * CT)
                kv_groups(b, 0, TT)

            def attention_slot(b, n):
                if n < 2:
                    kv_groups(b, TT + n * CT, TT + (n + 1) * CT)
                i = n - 2
                if 0 <= i < TT:
                    q_tile(b, i)
                if 1 <= i <= TT:
                    turn(b, i - 1)
                if 0 <= i < TT:
                    scores(b, i)
                if 1 <= i <= TT:
                    attend(b, i - 1)
                if n == 11:
                    pe.wait_ge(x1_attn, b * TT + TT)
                    norm_mean(PY, x1)
                if n == 12:
                    norm_var(b * 3 + 2, spare)
                if n == 13:
                    gate_scores(b)
                if n == 14:
                    gate_turn(b)
                if n == 15:
                    second_biases(b)

            def expert_step(b, e, chunk, p, lag=True):
                ec = (b * NE + e) * NH + chunk
                cols = slice(chunk * HALF, (chunk + 1) * HALF)
                if p == 1:
                    pe.wait_ge(y_read, ec + 1)
                    if chunk == 0:
                        pe.wait_ge(sel_copy, b * NE + (e + 1))
                    pe.matmul(banks(PY), selc, gt[:, cols], start=True, stop=True).then_inc(gbc_full, 1)
                w1 = ring[:, p % RING, 0:CT * 2 * P].rearrange("p (t n) -> p t n", t=CT)
                pe.wait_ge(w_full[p % RING], ec * (16 * PAIRS // RING) + 16 * (p // RING + 1))
                pe.wait_ge(gelu_done, ec * (2 * PAIRS) + (2 * p + 1))
                for s in range(2):
                    for c in range(CT):
                        mm = pe.matmul(banks(PH + s), w1[:, c, s * P:(s + 1) * P], xln[:, c, cols],
                                       start=(c == 0), stop=(c == CT - 1))
                    mm.then_inc(l1_full, 1)
                if p == 0:
                    if lag:
                        expert_second(ec - 1, PAIRS - 1)
                else:
                    expert_second(ec, p - 1)

            def expert_second(ec, p):
                w2 = ring[:, p % RING, CT * 2 * P:].rearrange("p (t n) -> p t n", t=2)
                if p == 0:
                    pe.wait_ge(gbc_copy, ec + 1)
                pe.wait_ge(gelu_done, ec * (2 * PAIRS) + (2 * p + 3))
                for o in range(CT):
                    for s in range(2):
                        mm = pe.matmul(banks(PY + o), w2[:, s, o * P:(o + 1) * P], hid[:, p % 2, s, :],
                                       start=(p == 0 and s == 0), stop=(p == PAIRS - 1 and s == 1))
                mm.then_inc(pair_used, 1)

            group_norm(0)
            for k in range(K):
                prepare(0, k)
                with pe.Fori(0, N) as n:
                    state_rows(0, k, n)
            scan_back(0)
            with pe.Fori(1, NB) as b:
                attention_start(b - 1)
                group_norm(b)
                for k in range(K):
                    prepare(b, k)
                    state_rows(b, k, 0)
                    for n in range(N):
                        if n + 1 < N:
                            state_rows(b, k, n + 1)
                        if k == 0:
                            attention_slot(b - 1, n)
                        else:
                            q = (k - 1) * N + n
                            if q == 0:
                                pe.wait_ge(b2_add, (b - 1) * (CT * NH) + CT * NH)
                            expert_step(b - 1, q // (NH * PAIRS), q // PAIRS % NH, q % PAIRS, q > 0)
                expert_second((b - 1) * E_B + (E_B - 1), PAIRS - 1)
                scan_back(b)
            attention_start(NB - 1)
            for n in range(N):
                attention_slot(NB - 1, n)
            pe.wait_ge(b2_add, NB * CT * NH)
            for e in range(NE):
                for chunk in range(NH):
                    for p in range(PAIRS):
                        expert_step(NB - 1, e, chunk, p, e + chunk + p > 0)
            expert_second(NB * E_B - 1, PAIRS - 1)


_INS = ["x", "xpw", "dtw", "chan", "wqkv", "gate_w", "gate_b", "b1", "b2", "wpk", "gmat", "lower"]


def kernel(**inputs):
    import numpy as np
    import concourse.bacc as bacc
    from concourse.bass_utils import run_bass_kernel_spmd

    a = {k: np.ascontiguousarray(v) for k, v in inputs.items()}
    proj = a["L0_conv_x_proj_weight"].transpose(2, 0, 1)
    rows = proj[:, :, R:]
    per_channel = [a["L0_conv_dt_projs_bias"].T,
                   a["L0_conv_A_logs"].reshape(K, C, N).transpose(1, 0, 2).reshape(C, K * N),
                   a["L0_conv_Ds"].reshape(K, C).T, a["L0_conv_ln_weight"][:, None], a["L0_conv_ln_bias"][:, None]]
    w1 = a["L1_ffn_w1"].reshape(NE, CT, P, PAIRS, 2 * P).transpose(0, 3, 2, 1, 4).reshape(NE * PAIRS, P, CT * 2 * P)
    w2 = a["L1_ffn_w2"].reshape(NE, PAIRS, 2, P, C).transpose(0, 1, 3, 2, 4).reshape(NE * PAIRS, P, 2 * C)
    groups = np.arange(C) // GROUP
    gmat = (groups[:, None] == groups[None]).astype(np.float32) / np.float32(GROUP)
    data = {
        "x": a["x"].reshape(NB, C, L),
        "xpw": np.concatenate([rows, rows, rows, proj[:, :, :R]], axis=2),
        "dtw": a["L0_conv_dt_projs_weight"].transpose(2, 0, 1),
        "chan": np.concatenate(per_channel, axis=1),
        "wqkv": np.stack([a["L1_attn_Wq"], a["L1_attn_Wk"], a["L1_attn_Wv"]], axis=1),
        "gate_w": a["L1_ffn_gate_w"],
        "gate_b": np.repeat(a["L1_ffn_gate_b"][None], P, axis=0),
        "b1": a["L1_ffn_b1"].reshape(NE, 2 * PAIRS, P).transpose(2, 0, 1).reshape(P, NE * 2 * PAIRS),
        "b2": a["L1_ffn_b2"],
        "wpk": np.concatenate([w1, w2], axis=2),
        "gmat": np.stack([gmat[j * P:(j + 1) * P, o * P:(o + 1) * P]
                          for j in range(CT) for o in range(CT) if abs(j - o) <= 1]),
        "lower": np.repeat(np.tril(np.ones((NE, NE), np.float32), -1)[None], P, axis=0),
    }
    nc = bacc.Bacc("TRN2", target_bir_lowering=False, num_devices=1)
    arrays, aps = {}, []
    for name in _INS:
        arr = np.ascontiguousarray(data[name])
        arrays[f"in_{name}"] = arr
        aps.append(nc.dram_tensor(f"in_{name}", arr.shape, mybir.dt.from_np(arr.dtype), kind="ExternalInput").ap())
    out = nc.dram_tensor("out_0", (NB, C, L), F32, kind="ExternalOutput").ap()
    build(nc, *aps, out)
    r = run_bass_kernel_spmd(nc, [arrays], core_ids=[0])
    return r.results[0]["out_0"].reshape(NB, C, HH, WW)
```

```python
from contextlib import ExitStack

import concourse.bass as bass
from concourse import mybir

F32 = mybir.dt.float32
BF16 = mybir.dt.bfloat16
ALU = mybir.AluOpType
ACT = mybir.ActivationFunctionType
AX = mybir.AxisListType

P = 128
NB, C, HH, WW = 4, 384, 32, 32
L = HH * WW
CT = C // P
HALF = 512
NH = L // HALF
K, N, R = 4, 16, 12
BC = 2 * N
TT = L // P
NE, HID = 4, 4 * C
PAIRS = HID // (2 * P)
GROUP = C // 32
EPS = 1e-5
MASKED = -1e30
RING = 3
SCALE = float(C) ** -0.5
DTB, ALOG, DSK, LNW, LNB, CHAN = 0, K, K + K * N, 2 * K + K * N, 2 * K + K * N + 1, 2 * K + K * N + 2


def build(nc, x, xpw, dtw, chan, wqkv, gate_w, gate_b, b1, b2, wpk, gmat, lower, out):
    with ExitStack() as ctx:
        def sb(name, shape, dt=F32):
            return ctx.enter_context(nc.sbuf_tensor(name, shape, dt))

        def sem(name):
            return ctx.enter_context(nc.semaphore(name))

        u = sb("u", [P, CT, L])
        dt = sb("dt", [P, CT, L])
        spare = sb("spare", [P, CT, L])
        dtu = sb("dtu", [P, CT, L])
        bcs = sb("bcs", [P, 2, L], BF16)
        xd = sb("xd", [P, L])
        tmp = sb("tmp", [P, CT, L])
        work = sb("work", [P, 3, CT, L])
        cbc = sb("cbc", [P, 2, L])
        acc = sb("acc", [P, CT, L])
        x1 = sb("x1", [P, CT, L])
        xln = sb("xln", [P, CT, L])
        ring = sb("ring", [P, RING, CT * 2 * P + 2 * C])
        hid = sb("hid", [P, 2, 2, HALF])
        qt = sb("qt", [P, CT, P])
        ytmp = sb("ytmp", [P, CT, HALF])
        gbc = sb("gbc", [P, HALF])
        small = sb("small", [P, L + C + NE * P + P])
        gt = small[0:NE, 0:L]
        b2_sb = small[0:NE, L:L + C]
        sel4 = small[0:NE, L + C:L + C + NE * P].rearrange("p (e n) -> p e n", e=NE)
        selc = small[0:NE, L + C + NE * P:]
        dtw_sb = small[3 * BC:3 * BC + R, 0:K * C].rearrange("p (k c) -> p k c", k=K)
        ident = sb("ident", [P, P])
        tri = sb("tri", [P, P])
        mean_w = sb("mean_w", [P, P])
        sel = sb("sel", [P, BC, P], BF16)
        xpw_sb = sb("xpw_sb", [P, CT, K, 3 * BC + R])
        ch = sb("ch", [P, CT, CHAN])
        nega = ch[:, :, ALOG:ALOG + K * N]
        dsum = sb("dsum", [P, CT])
        b1_sb = sb("b1_sb", [P, NE * 2 * PAIRS])
        gw_sb = sb("gw_sb", [P, CT, NE])
        gb_sb = sb("gb_sb", [P, NE])
        low_sb = sb("low_sb", [P, NE, NE])
        bn = sb("bn", [P, CT, NH, 6])
        mv = sb("mv", [P, CT, 2])
        gmean = sb("gmean", [P, CT])
        gvar = sb("gvar", [P, CT])
        grstd = sb("grstd", [P, CT])
        rmax = sb("rmax", [P, 2])
        nbias = sb("nbias", [P, 2])
        rsum = sb("rsum", [P, 2])
        rinv = sb("rinv", [P, 2])
        eps_c = sb("eps_c", [P, 1])
        one_c = sb("one_c", [P, 1])

        ps = ctx.enter_context(nc.psum_tensor("ps", [P, 8 * HALF], F32))

        def banks(a, n=1):
            return ps[:, a * HALF:(a + n) * HALF]

        PB, PM, PH, PY = 0, 2, 3, 5
        PO = 7
        BLOCKS = [(j, o) for j in range(CT) for o in range(CT) if abs(j - o) <= 1]
        gm_w = tmp[:, 0, 0:len(BLOCKS) * P].rearrange("p (g n) -> p g n", n=P)
        da, dbu, h = (work[:, i] for i in range(3))
        scan_rstd = tmp[:, 0, :]
        kt = tmp
        vv = spare[:].rearrange("p t l -> p (t l)").rearrange("p (s c) -> p s c", c=C)
        prob = [hid[:, i].rearrange("p s n -> p (s n)") for i in range(2)]
        gs, gp, rank = (spare[:, 0, i * TT * NE:(i + 1) * TT * NE].rearrange("p (t e) -> p t e", e=NE) for i in range(3))
        gr, gi = (spare[:, 0, (12 + i) * TT:(13 + i) * TT] for i in range(2))
        cgt, ceq = (spare[:, 1, i * TT * NE * NE:(i + 1) * TT * NE * NE].rearrange("p (t e f) -> p t e f", e=NE, f=NE)
                    for i in range(2))
        rstd = prob[0]
        pt = ytmp[:].rearrange("p t n -> p (t n)")[:, 0:L]
        wq_sb = ring[:].rearrange("p r n -> p (r n)")[:, 0:CT * 3 * C].rearrange("p (t m n) -> p t m n", t=CT, m=3)

        c_load = sem("const_loaded")
        b1_full = sem("first_biases_loaded")
        c_mem = sem("const_zeroed")
        c_pool = sem("const_built")
        c_exp = sem("const_exp")
        c_dve = sem("const_scaled")
        x_full = sem("x_loaded")
        xres_full = sem("residual_loaded")
        gn_step = sem("gn_step")
        gm_full = sem("group_blocks_loaded")
        gn_rstd = sem("gn_rstd")
        u_ready = sem("u_normed")
        acc_init = sem("acc_started")
        misc_full = sem("misc_full")
        misc_free = sem("misc_free")
        split_step = sem("split_step")
        sp_exp = sem("softplus_exp")
        sp_ln = sem("softplus_log")
        sp_corr = sem("softplus_corrected")
        sp_one = sem("softplus_rounded")
        dt_full = sem("dt_full")
        dt_read = sem("dt_read")
        dt_abs = sem("dt_abs")
        dt_dve = sem("dt_step_vector")
        dt_pool = sem("dt_step_gpsimd")
        dtu_dve = sem("dtu_vector")
        dtu_pool = sem("dtu_gpsimd")
        b_full = sem("b_row_full")
        dbu_done = sem("dbu_done")
        da_done = sem("da_done")
        scan_done = sem("scan_done")
        hc_done = sem("hc_done")
        acc_done = sem("acc_done")
        acc_pe = sem("acc_tensor")
        ln_mean = sem("ln_mean")
        ln_cent = sem("ln_centred")
        ln_sq = sem("ln_squared")
        ln_var = sem("ln_var")
        ln_log = sem("ln_log")
        ln_rstd = sem("ln_rstd")
        ln_out = sem("ln_out")
        ssm_act = sem("ssm_activated")
        x1_ssm = sem("x1_from_scan")
        wq_full = sem("wqkv_loaded")
        kv_full = sem("kv_full")
        kv_copy = sem("kv_copied")
        q_full = sem("q_full")
        q_copy = sem("q_copied")
        s_full = sem("scores_full")
        sm_step = sem("softmax_step")
        p_exp = sem("probs_exp")
        p_norm = sem("probs_normed")
        pt_full = sem("probs_turned")
        pt_copy = sem("probs_copied")
        o_full = sem("attn_out_full")
        x1_attn = sem("x1_from_attention")
        g_full = sem("gate_scores_full")
        g_step = sem("gate_step")
        g_exp = sem("gate_exp")
        g_norm = sem("gate_normed")
        g_turn = sem("gate_turned")
        g_copy = sem("gate_copied")
        b2_load = sem("second_biases_loaded")
        b2_full = sem("b2_full")
        b2_add = sem("b2_added")
        w_full = [sem(f"weights_loaded_{i}") for i in range(RING)]
        pair_used = sem("pair_used")
        l1_full = sem("hidden_full")
        gelu_done = sem("gelu_done")
        sel_copy = sem("expert_row_selected")
        gbc_full = sem("gate_row_full")
        gbc_copy = sem("gate_row_copied")
        y_read = sem("expert_out_read")
        x1_ffn = sem("x1_from_experts")
        out_done = sem("out_stored")

        CONST_LOADS = 6
        GN_STEPS, SPLIT_STEPS, GATE_STEPS = 12, 6, 14
        MISC_K = NH + 2 * N
        SUM_PE = 2
        AHEAD = N - 6
        GN_K = 1
        T_NORM, T_KV, T_TILE, T_GATE = 3, 4, 7, 16
        SIDE = T_GATE + 4
        KV = TT + CT * NH
        E_B = NE * NH
        PAIRS_B = E_B * PAIRS

        block = ctx.enter_context(nc.Block())

        def half(ap, s):
            return ap[:, :, s * HALF:(s + 1) * HALF]

        def tiles(ap):
            return ap.unsqueeze(1).broadcast_to([P, CT, HALF])

        def kv_part(m):
            t, parts = m - T_KV, T_TILE - T_KV
            return t * KV // parts, (t + 1) * KV // parts

        def is_int(i, value):
            return isinstance(i, int) and i == value

        def first_of_all(b, k):
            return is_int(b, 0) and k == 0

        def following(b, k):
            if k + 1 < K:
                return b, k + 1
            return None if is_int(b, NB - 1) else (b + 1, 0)

        def c_use(b, k, n):
            late = n - (AHEAD + 1) if isinstance(n, int) else 0
            halves = min(max(late, 0), NH) if following(b, k) else 0
            sums = 0 if is_int(b, NB - 1) else 2 if k > GN_K else max(late - NH, 0) if k == GN_K else 0
            return b * (K * MISC_K + 2) + n * 2 + (2 + k * MISC_K + NH + halves + sums)

        def rows_use(b, k, s):
            if first_of_all(b, k):
                return 2 + s
            return (c_use(b, k - 1, AHEAD + 1 + s) if k else c_use(b - 1, K - 1, AHEAD + 1 + s)) + 2

        def sums_use(b, stat):
            return stat if is_int(b, 0) else c_use(b - 1, GN_K, AHEAD + 3 + stat) + 2

        def pairs_at(m):
            def before(m):
                return min(m - SIDE + max(0, m // 8 - 3), PAIRS_B)

            assert before(K * N - 1) < before(K * N) == PAIRS_B
            return range(before(m), before(m + 1))

        def rev(ap, k):
            return ap[:, ::-1] if k >= 2 else ap

        def by_rows(ap, k):
            return ap.rearrange("p (w h) -> p h w", w=WW) if k % 2 else ap.rearrange("p (h w) -> p h w", w=WW)

        def rows(ap):
            return ap.rearrange("p (h w) -> p h w", w=WW)


        @block.sync
        def _(sp):
            for dst, src in (
                (xpw_sb[:], xpw.rearrange("(t p) k m -> p t k m", p=P)),
                (dtw_sb, dtw),
                (ch[:], chan.rearrange("(t p) m -> p t m", p=P)),
                (gw_sb[:], gate_w.rearrange("(t p) m -> p t m", p=P)),
                (gb_sb[:], gate_b), (low_sb[:], lower),
            ):
                sp.dma_start(dst, src).then_inc(c_load, 16)
            sp.dma_start(b1_sb[:], b1).then_inc(b1_full, 16)

            def image(b):
                return x[bass.ds(b, 1)].rearrange("b (t p) l -> p (b t) l", p=P)

            def experts(b):
                with sp.Fori(0, NE) as e:
                    for chunk in range(NH):
                        for p in range(PAIRS):
                            sp.wait_ge(pair_used, (b * NE + e) * (NH * PAIRS) + (chunk * PAIRS + p + 1))
                            sp.dma_start(ring[:, p % RING, :],
                                         wpk[bass.ds(e * PAIRS + p, 1)].rearrange("g p n -> p (g n)")
                                         ).then_inc(w_full[p % RING], 16)

            def attention_weights(b):
                sp.wait_ge(pair_used, b * PAIRS_B + RING)
                sp.dma_start(wq_sb, wqkv.rearrange("(t p) m n -> p t m n", p=P)).then_inc(wq_full, 16)

            def residual(b):
                sp.dma_start(spare[:], image(b)).then_inc(xres_full, 16)

            def store(b):
                sp.wait_ge(x1_ffn, b * E_B + (E_B + 1))
                sp.dma_start(out[bass.ds(b, 1)].rearrange("b (t p) l -> p (b t) l", p=P), x1[:]).then_inc(out_done, 16)

            def group_blocks():
                sp.dma_start(gm_w, gmat.rearrange("g p n -> p g n")).then_inc(gm_full, 16)

            def beside(b):
                attention_weights(b - 1)
                sp.wait_ge(q_full, (b - 1) * TT + TT)
                sp.dma_start(b2_sb, b2).then_inc(b2_load, 16)
                sp.wait_ge(g_copy, b)
                if is_int(b, NB - 1):
                    residual(b)
                else:
                    group_blocks()
                    sp.dma_start(spare[:], image(b + 1)).then_inc(x_full, 16)
                experts(b - 1)
                if not is_int(b, NB - 1):
                    sp.wait_ge(u_ready, (b + 1) * CT + CT)
                    residual(b)
                store(b - 1)

            group_blocks()
            sp.dma_start(u[:], image(0)).then_inc(x_full, 16)
            sp.wait_ge(x_full, 16)
            sp.dma_start(spare[:], image(1)).then_inc(x_full, 16)
            sp.wait_ge(dtu_dve, (GN_K + 1) * 2 + 1)
            group_blocks()
            sp.wait_ge(u_ready, 2 * CT)
            residual(0)
            with sp.Fori(1, NB - 1) as b:
                beside(b)
            beside(NB - 1)
            attention_weights(NB - 1)
            sp.wait_ge(q_full, NB * TT)
            sp.dma_start(b2_sb, b2).then_inc(b2_load, 16)
            experts(NB - 1)
            store(NB - 1)
            sp.wait_ge(out_done, 16 * NB + 1)

        @block.gpsimd
        def _(pool):
            for t, value in ((ident[:], 0.0), (tri[:], 0.0), (sel[:], 0.0), (sel4, 0.0), (mean_w[:], 1.0 / C),
                             (eps_c[:], EPS), (one_c[:], 1.0)):
                pool.memset(t, value).then_inc(c_mem, 1)
            pool.wait_ge(c_mem, 7)
            pool.affine_select(out=ident[:], in_=ident[:], compare_op=ALU.not_equal, fill=1.0, base=0,
                               pattern=[[-1, P]], channel_multiplier=1).then_inc(c_pool, 1)
            pool.affine_select(out=tri[:], in_=tri[:], compare_op=ALU.is_ge, fill=MASKED, base=0,
                               pattern=[[-1, P]], channel_multiplier=1).then_inc(c_pool, 1)
            pool.affine_select(out=sel4, in_=sel4, compare_op=ALU.not_equal, fill=1.0, base=0,
                               pattern=[[-1, NE], [0, P]], channel_multiplier=1).then_inc(c_pool, 1)
            for part in range(3):
                pool.affine_select(out=sel[:], in_=sel[:], compare_op=ALU.not_equal, fill=1.0, base=-BC * part,
                                   pattern=[[-1, BC], [0, P]], channel_multiplier=1).then_inc(c_pool, 1)
                pool.wait_ge(c_pool, 4 + part)

            def image(b):
                for k in range(K):
                    kk = b * K + k
                    d, step = dt[:, 1, :], dtu[:, 1, :]
                    pool.wait_ge(sp_ln, kk * CT + 2)
                    pool.wait_ge(sp_corr, kk * CT + 2)
                    pool.tensor_tensor(d, d, step, ALU.add).then_inc(dt_pool, 1)
                    pool.wait_ge(dt_pool, kk + 1)
                    pool.tensor_tensor(step, d, u[:, 1, :], ALU.mult).then_inc(dtu_pool, 1)

                    def products(n, par):
                        for j in range(CT):
                            if j == 0:
                                pool.wait_ge(misc_free, c_use(b, k, n) + 3)
                            pool.wait_ge(scan_done, (kk * N + n) * CT + (CT + j + 1))
                            pool.tensor_tensor(h[:, j, :], h[:, j, :], cbc[:, par, :], ALU.mult).then_inc(hc_done, 1)

                    with pool.Fori(0, AHEAD, 2) as n:
                        products(n, 0)
                        products(n + 1, 1)
                    for n in range(AHEAD, N):
                        products(n, n % 2)

            with pool.Fori(0, NB - 1) as b:
                image(b)
            image(NB - 1)

        @block.scalar
        def _(act):
            act.wait_ge(c_load, 16 * CONST_LOADS)
            act.wait_ge(b1_full, 16)
            act.wait_ge(c_mem, 7)
            act.activation(nega, ch[:, :, ALOG:ALOG + K * N], ACT.Exp).then_inc(c_exp, 1)

            def norm_squares(c, src, sq):
                for s in range(NH):
                    act.wait_ge(ln_cent, c * NH + (s + 1))
                    act.activation(half(sq, s), half(src, s), ACT.Square).then_inc(ln_sq, 1)

            def norm_rstd(c, r):
                for s in range(NH):
                    act.wait_ge(ln_var, c * NH + (s + 1))
                    act.activation(r[:, s * HALF:(s + 1) * HALF], banks(PH + s), ACT.Ln,
                                   bias=eps_c[:, 0:1]).then_inc(ln_log, 1)
                for s in range(NH):
                    part = r[:, s * HALF:(s + 1) * HALF]
                    act.wait_ge(ln_log, c * NH + (s + 1))
                    act.activation(part, part, ACT.Exp, scale=-0.5).then_inc(ln_rstd, 1)

            def group_mean(b):
                act.wait_ge(misc_full, sums_use(b, 0) + 1)
                act.activation(gmean[:], banks(PM)[:, 0:CT], ACT.Copy).then_inc(misc_free, 1)

            def group_rstd(b):
                act.wait_ge(misc_full, sums_use(b, 1) + 1)
                act.activation(gvar[:], banks(PM)[:, 0:CT], ACT.Ln, bias=eps_c[:, 0:1]).then_inc(misc_free, 1)
                act.wait_ge(misc_free, sums_use(b, 1) + 2)
                act.activation(grstd[:], gvar[:], ACT.Exp, scale=-0.5).then_inc(gn_rstd, 1)

            def copy_rows(b, k, s):
                if s == 0:
                    act.wait_ge(split_step, (b * K + k) * SPLIT_STEPS + 1)
                act.wait_ge(misc_full, rows_use(b, k, s) + 1)
                act.activation(xd[0:3 * BC + R, s * HALF:(s + 1) * HALF], banks(PM)[0:3 * BC + R, :],
                               ACT.Copy).then_inc(misc_free, 1)

            def step_tile(b, k, j):
                kk = b * K + k
                if not first_of_all(b, k):
                    act.wait_ge(da_done, kk * (N * CT) + (j + 1 - CT))
                act.wait_ge(dt_full, kk * CT + (j + 1))
                act.activation(dt[:, j, :], banks(PB, 2), ACT.Identity,
                               bias=ch[:, j, DTB + k:DTB + k + 1]).then_inc(dt_read, 1)

            def step_exp(b, k, j):
                kk = b * K + k
                act.wait_ge(dt_read, kk * CT + (j + 1))
                act.activation(tmp[:, j, :], dt[:, j, :], ACT.Abs).then_inc(dt_abs, 1)
                act.wait_ge(dt_abs, kk * CT + (j + 1))
                act.activation(tmp[:, j, :], tmp[:, j, :], ACT.Exp, scale=-1.0).then_inc(sp_exp, 1)

            def steps(b, k):
                kk = b * K + k
                step_exp(b, k, 0)
                for j in range(1, CT):
                    step_tile(b, k, j)
                    step_exp(b, k, j)
                c_row(b, k, 0, 0)
                act.wait_ge(dbu_done, kk * (N * CT) + 1)
                for j in range(CT):
                    act.wait_ge(sp_exp, kk * CT + (j + 1))
                    act.activation(dtu[:, j, :], tmp[:, j, :], ACT.Ln, bias=one_c[:, 0:1]).then_inc(sp_ln, 1)
                act.wait_ge(sp_corr, kk * CT + CT)

            def decay(b, k, n, j):
                if isinstance(n, int) and n == 0:
                    if j == 1:
                        act.wait_ge(dt_pool, (b * K + k) + 1)
                    else:
                        act.wait_ge(dt_dve, (b * K + k) * 2 + (j // 2 + 1))
                act.wait_ge(scan_done, ((b * K + k) * N + n) * CT + (j + 1))
                act.wait_ge(c_dve, 2)
                act.activation(by_rows(da[:, j, :], k), rows(dt[:, j, :]), ACT.Exp,
                               scale=nega[:, j, bass.ds(n + k * N, 1)]).then_inc(da_done, 1)

            def c_half(b, k, n, par, s):
                if s == 0 and not (first_of_all(b, k) and isinstance(n, int) and n == 0):
                    act.wait_ge(hc_done, ((b * K + k) * N + n - 1) * CT + 1)
                act.wait_ge(misc_full, c_use(b, k, n) + (s + 1))
                act.activation(by_rows(cbc[:, par, :], k)[:, s * (HH // NH):(s + 1) * (HH // NH), :],
                               rows(banks(PM)), ACT.Copy).then_inc(misc_free, 1)

            def decays(b, k, n):
                after = following(b, k) if isinstance(n, int) else None
                for j in range(CT):
                    decay(b, k, n, j)
                    if after and n == N - 1 and j == 0:
                        step_tile(*after, 0)
                if after and n == N - 1:
                    steps(*after)
                if after and n - (AHEAD + 1) in range(NH):
                    copy_rows(*after, n - (AHEAD + 1))
                if k == GN_K and not is_int(b, NB - 1):
                    if is_int(n, AHEAD + 3):
                        group_mean(b + 1)
                    if is_int(n, AHEAD + 4):
                        group_rstd(b + 1)

            def state(b, k, n, par):
                decays(b, k, n)
                if not is_int(n, N - 1):
                    c_row(b, k, n + 1, 1 - par)

            def c_row(b, k, n, par):
                for s in range(NH):
                    c_half(b, k, n, par, s)

            def scan_gelu(b):
                for j in range(CT):
                    act.wait_ge(ln_out, b * (3 * NH) + NH)
                    act.activation(x1[:, j, :], x1[:, j, :], ACT.Gelu, scale=ch[:, j, LNW:LNW + 1],
                                   bias=ch[:, j, LNB:LNB + 1]).then_inc(ssm_act, 1)

            def kv_copies(b, i0, i1):
                for i in range(i0, i1):
                    act.wait_ge(kv_full, b * KV + (i + 1))
                    src = banks(PH + i % 2)
                    if i < TT:
                        act.activation(vv[:, i, :], src[:, 0:C], ACT.Copy).then_inc(kv_copy, 1)
                    else:
                        o, s = (i - TT) // NH, (i - TT) % NH
                        act.activation(kt[:, o, s * HALF:(s + 1) * HALF], src, ACT.Copy).then_inc(kv_copy, 1)

            def q_tile(b, i):
                act.wait_ge(q_full, b * TT + (i + 1))
                act.activation(qt[:], banks(PO)[:, 0:C].rearrange("p (t n) -> p t n", t=CT), ACT.Copy).then_inc(q_copy, 1)

            def probs(b, i):
                w = (i + 1) * P
                act.wait_ge(sm_step, b * (3 * TT) + 3 * (i + 1))
                if i >= 2:
                    act.wait_ge(pt_full, b * TT + (i - 1))
                act.activation(prob[i % 2][:, 0:w], banks(PY, 2)[:, 0:w], ACT.Exp, scale=SCALE,
                               bias=nbias[:, i % 2:i % 2 + 1], accum_out=rsum[:, i % 2:i % 2 + 1]).then_inc(p_exp, 1)

            def turned(b, i):
                w = (i + 1) * P
                act.wait_ge(pt_full, b * TT + (i + 1))
                if i >= 1:
                    act.wait_ge(o_full, b * TT + i)
                act.activation(pt[:, 0:w], banks(PH, 2)[:, 0:w], ACT.Copy).then_inc(pt_copy, 1)

            def gate_exp(b):
                act.wait_ge(g_step, b * GATE_STEPS + 3)
                act.activation(gp, gs, ACT.Exp).then_inc(g_exp, 1)

            def gate_rows(b):
                act.wait_ge(g_turn, b + 1)
                act.activation(gt, banks(PY, 2)[0:NE, :], ACT.Copy).then_inc(g_copy, 1)

            def gate_row(b, q):
                if q % PAIRS != 1:
                    return
                ec = q // PAIRS
                act.wait_ge(gbc_full, b * E_B + (ec + 1))
                act.activation(gbc[:], banks(PY + CT - 1), ACT.Copy).then_inc(gbc_copy, 1)

            def activate(b, q):
                e, chunk, p = q // (NH * PAIRS), q // PAIRS % NH, q % PAIRS
                if p == 0 and chunk == 0:
                    act.activation(selc, sel4[:, e, :], ACT.Copy).then_inc(sel_copy, 1)
                act.wait_ge(pair_used, b * PAIRS_B + (q + RING - 1))
                for s in range(2):
                    col = 2 * (e * PAIRS + p) + s
                    act.wait_ge(l1_full, b * (2 * PAIRS_B) + (2 * q + s + 1))
                    act.activation(hid[:, p % 2, s, :], banks(PH + s), ACT.Gelu,
                                   bias=b1_sb[:, col:col + 1]).then_inc(gelu_done, 1)

            def side(b, m):
                if m == 0:
                    norm_squares(b * 3, x1, tmp)
                if m == 1:
                    norm_rstd(b * 3, scan_rstd)
                if m == 2:
                    scan_gelu(b)
                if m == T_NORM:
                    norm_squares(b * 3 + 1, xln, tmp)
                    norm_rstd(b * 3 + 1, rstd)
                if T_KV <= m <= T_TILE:
                    first, last = kv_part(m)
                    kv_copies(b, max(first - 2, 0), min(last - 2, KV))
                i = m - T_TILE
                if i == 0:
                    q_tile(b, 0)
                if 1 <= i + 1 < TT:
                    q_tile(b, i + 1)
                if 1 <= i <= TT:
                    turned(b, i - 1)
                if 0 <= i < TT:
                    probs(b, i)
                if m == T_GATE:
                    norm_squares(b * 3 + 2, xln, spare)
                    norm_rstd(b * 3 + 2, rstd)
                if m == T_GATE + 1:
                    gate_exp(b)
                if m == T_GATE + 2:
                    gate_rows(b)

            def beside(b):
                for k in range(K):
                    for n in range(N):
                        m = k * N + n
                        if m < SIDE:
                            state(b, k, n, n % 2)
                            side(b - 1, m)
                            continue
                        decays(b, k, n)
                        for i, q in enumerate(pairs_at(m)):
                            activate(b - 1, q)
                            if i == 0 and n < N - 1:
                                c_row(b, k, n + 1, 1 - n % 2)
                            gate_row(b - 1, q)

            group_mean(0)
            group_rstd(0)
            copy_rows(0, 0, 0)
            copy_rows(0, 0, 1)
            step_tile(0, 0, 0)
            steps(0, 0)
            for k in range(K):
                state(0, k, 0, 0)
                state(0, k, 1, 1)
                with act.Fori(2, AHEAD, 2) as n:
                    state(0, k, n, 0)
                    state(0, k, n + 1, 1)
                for n in range(AHEAD, N):
                    state(0, k, n, n % 2)
            with act.Fori(1, NB - 1) as b:
                beside(b)
            beside(NB - 1)
            for m in range(SIDE):
                side(NB - 1, m)
            for q in range(PAIRS_B):
                activate(NB - 1, q)
                gate_row(NB - 1, q)

        @block.vector
        def _(dve):
            for s in (x1_ssm, split_step, dtu_dve, misc_free, hc_done, gelu_done, dbu_done, y_read, x1_ffn, out_done):
                dve.sem_inc(s, 1)
            dve.sem_inc(scan_done, CT)
            dve.sem_inc(acc_done, CT)
            dve.sem_inc(acc_pe, SUM_PE)
            dve.sem_inc(pair_used, RING)
            dve.wait_ge(c_exp, 1)
            dve.tensor_scalar(nega, nega, -1.0, None, ALU.mult).then_inc(c_dve, 1)
            dve.tensor_reduce(dsum[:], ch[:, :, DSK:DSK + K], AX.X, ALU.add).then_inc(c_dve, 1)
            dve.wait_ge(c_dve, 2)

            def norm_centre(c, src, dst, bank):
                for s in range(NH):
                    dve.wait_ge(ln_mean, c * NH + (s + 1))
                    dve.tensor_tensor(half(dst, s), half(src, s), tiles(banks(bank + s)), ALU.subtract
                                      ).then_inc(ln_cent, 1)

            def norm_scale(c, dst, r):
                for s in range(NH):
                    dve.wait_ge(ln_rstd, c * NH + (s + 1))
                    dve.tensor_tensor(half(dst, s), half(dst, s), tiles(r[:, s * HALF:(s + 1) * HALF]), ALU.mult
                                      ).then_inc(ln_out, 1)

            def channel_stats(b, src):
                g0 = b * GN_STEPS
                dve.wait_ge(x_full, b * 16 + 16)
                for j in range(CT):
                    for s in range(NH):
                        dve.bn_stats(bn[:, j, s, :], src[:, j, s * HALF:(s + 1) * HALF]).then_inc(gn_step, 1)
                dve.wait_ge(gn_step, g0 + 6)
                dve.memset(gvar[:], 0.0)
                for j in range(CT):
                    dve.bn_aggr(mv[:, j, :], bn[:, j, :, :]).then_inc(gn_step, 1)

            def spread(b):
                g0 = b * GN_STEPS
                dve.wait_ge(misc_free, sums_use(b, 0) + 2)
                dve.tensor_tensor(gvar[:], mv[:, :, 0], gmean[:], ALU.subtract).then_inc(gn_step, 1)
                dve.wait_ge(gn_step, g0 + 10)
                dve.tensor_tensor(gvar[:], gvar[:], gvar[:], ALU.mult).then_inc(gn_step, 1)
                dve.wait_ge(gn_step, g0 + 11)
                dve.tensor_tensor(mv[:, :, 1], mv[:, :, 1], gvar[:], ALU.add).then_inc(gn_step, 1)

            def norm_image(b, src):
                dve.wait_ge(gn_rstd, b + 1)
                for j in range(CT):
                    dve.tensor_scalar(u[:, j, :], src[:, j, :], gmean[:, j:j + 1], grstd[:, j:j + 1],
                                      ALU.subtract, ALU.mult).then_inc(u_ready, 1)

            def start_sum(b):
                for j in range(CT):
                    dve.wait_ge(u_ready, b * CT + (j + 1))
                    dve.tensor_scalar(acc[:, j, :], u[:, j, :], dsum[:, j:j + 1], None, ALU.mult).then_inc(acc_init, 1)

            def split_rows(b, k):
                s0 = (b * K + k) * SPLIT_STEPS
                S, rows3 = bcs[:, k % 2, :], 3 * BC
                rest = dbu[:, 0, :]
                left = 0 if first_of_all(b, k) else N - AHEAD - 4
                dve.wait_ge(scan_done, (b * K + k) * (N * CT) + (1 - left) * CT)
                dve.wait_ge(misc_free, rows_use(b, k, NH - 1) + 2)
                dve.tensor_copy(S[0:rows3], xd[0:rows3]).then_inc(split_step, 1)
                dve.wait_ge(split_step, s0 + 2)
                dve.tensor_tensor(rest[0:rows3], xd[0:rows3], S[0:rows3], ALU.subtract).then_inc(split_step, 1)
                dve.wait_ge(split_step, s0 + 3)
                dve.tensor_copy(S[BC:2 * BC], rest[BC:2 * BC]).then_inc(split_step, 1)
                dve.tensor_copy(S[2 * BC:rows3], rest[2 * BC:rows3]).then_inc(split_step, 1)
                dve.wait_ge(split_step, s0 + 5)
                dve.tensor_tensor(rest[2 * BC:rows3], rest[2 * BC:rows3], S[2 * BC:rows3], ALU.subtract).then_inc(split_step, 1)
                dve.wait_ge(split_step, s0 + 6)
                dve.tensor_copy(S[2 * BC:rows3], rest[2 * BC:rows3]).then_inc(split_step, 1)
                dve.wait_ge(split_step, s0 + 7)

            def correction(b, k, j):
                kk = b * K + k
                dve.wait_ge(scan_done, kk * (N * CT) + CT)
                dve.wait_ge(sp_exp, kk * CT + (j + 1))
                dve.tensor_scalar(dbu[:, j, :], tmp[:, j, :], 1.0, -1.0, ALU.add, ALU.add).then_inc(sp_one, 1)
                dve.wait_ge(sp_one, kk * (2 * CT) + (2 * j + 1))
                dve.tensor_tensor(dbu[:, j, :], tmp[:, j, :], dbu[:, j, :], ALU.subtract).then_inc(sp_one, 1)
                dve.wait_ge(sp_one, kk * (2 * CT) + (2 * j + 2))
                dve.scalar_tensor_tensor(out=dt[:, j, :], in0=dt[:, j, :], scalar=0.0, in1=dbu[:, j, :],
                                         op0=ALU.max, op1=ALU.add).then_inc(sp_corr, 1)

            def steps(b, k):
                kk = b * K + k
                for i, j in enumerate((0, 2)):
                    d, step = dt[:, j, :], dtu[:, j, :]
                    dve.wait_ge(sp_ln, kk * CT + (j + 1))
                    dve.wait_ge(sp_corr, kk * CT + (j + 1))
                    dve.tensor_tensor(d, d, step, ALU.add).then_inc(dt_dve, 1)
                    dve.wait_ge(dt_dve, kk * 2 + (i + 1))
                    dve.tensor_tensor(step, d, u[:, j, :], ALU.mult).then_inc(dtu_dve, 1)

            def inputs(b, k, n, first=False):
                g = (b * K + k) * N + n
                for j in range(CT):
                    if first:
                        if j == 1:
                            dve.wait_ge(dtu_pool, (b * K + k) + 1)
                        else:
                            dve.wait_ge(dtu_dve, (b * K + k) * 2 + (j // 2 + 2))
                    if j == 0:
                        dve.wait_ge(b_full, g + 1)
                    dve.wait_ge(scan_done, g * CT + (j + 1))
                    dve.tensor_tensor(by_rows(dbu[:, j, :], k), rows(dtu[:, j, :]), rows(banks(PB, 2)),
                                      ALU.mult).then_inc(dbu_done, 1)

            def scans(b, k, n, lag=False):
                g = (b * K + k) * N + n
                for j in range(CT):
                    if j == SUM_PE and lag:
                        last_sum(k, n - 1)
                    dve.wait_ge(da_done, g * CT + (j + 1))
                    dve.wait_ge(dbu_done, g * CT + (j + 2))
                    if is_int(b, 0) and j < SUM_PE:
                        dve.wait_ge(acc_pe, g * SUM_PE + (j + 1))
                    else:
                        dve.wait_ge(acc_done, g * CT + (j + 1))
                    dve.tensor_tensor_scan(rev(h[:, j, :], k), rev(da[:, j, :], k), rev(dbu[:, j, :], k),
                                           0.0, ALU.mult, ALU.add).then_inc(scan_done, 1)

            def last_sum(k, n):
                j, g = SUM_PE, k * N + n
                if is_int(g, 0):
                    dve.wait_ge(acc_init, CT)
                dve.wait_ge(hc_done, g * CT + (j + 2))
                dve.tensor_tensor(rows(acc[:, j, :]), rows(acc[:, j, :]), by_rows(h[:, j, :], k),
                                  ALU.add).then_inc(acc_done, CT)

            def sums(b, k, n):
                if is_int(b, 0):
                    if n == N - 1:
                        if k == K - 1:
                            dve.wait_ge(acc_pe, K * N * SUM_PE + SUM_PE)
                            dve.tensor_copy(acc[:, 0:SUM_PE, :], banks(PH, SUM_PE * NH).rearrange("p (t l) -> p t l", l=L))
                        last_sum(k, n)
                    return
                g = (b * K + k) * N + n
                for j in range(CT):
                    if k == 0 and is_int(n, 0):
                        dve.wait_ge(acc_init, b * CT + (j + 1))
                    dve.wait_ge(hc_done, g * CT + (j + 2))
                    dve.tensor_tensor(rows(acc[:, j, :]), rows(acc[:, j, :]), by_rows(h[:, j, :], k),
                                      ALU.add).then_inc(acc_done, 1)

            def slot(b, k, n, side):
                after = following(b, k)
                more = not is_int(b, NB - 1)
                scans(b, k, n, is_int(b, 0))
                side(0)
                if after and n == AHEAD and k == K - 1:
                    dve.wait_ge(dtu_pool, b * K + K)
                    dve.wait_ge(dtu_dve, b * (2 * K) + (2 * K + 1))
                    norm_image(b + 1, spare)
                if after and n == AHEAD + 3:
                    split_rows(*after)
                if n + 1 < N:
                    inputs(b, k, n + 1)
                side(1)
                if after and n == N - 1:
                    correction(*after, 0)
                    correction(*after, 1)
                sums(b, k, n)
                if more and k == GN_K and n == AHEAD + 1:
                    channel_stats(b + 1, spare)
                if more and k == GN_K and n == AHEAD + 3:
                    spread(b + 1)
                if after and n == N - 1:
                    correction(*after, 2)
                    steps(*after)
                side(2)

            def scan_residual(b):
                dve.wait_ge(xres_full, b * 16 + 16)
                for j in range(CT):
                    dve.wait_ge(ssm_act, b * CT + (j + 1))
                    dve.tensor_tensor(x1[:, j, :], x1[:, j, :], spare[:, j, :], ALU.add).then_inc(x1_ssm, 1)

            def maximum(b, i):
                w, s0, r = (i + 1) * P, b * (3 * TT), i % 2
                sc = banks(PY, 2)
                dve.wait_ge(s_full, b * TT + (i + 1))
                dve.tensor_tensor(sc[:, i * P:w], sc[:, i * P:w], tri[:], ALU.add).then_inc(sm_step, 1)
                dve.wait_ge(sm_step, s0 + (3 * i + 1))
                dve.tensor_reduce(rmax[:, r:r + 1], sc[:, 0:w], AX.X, ALU.max).then_inc(sm_step, 1)
                dve.wait_ge(sm_step, s0 + (3 * i + 2))
                dve.tensor_scalar(nbias[:, r:r + 1], rmax[:, r:r + 1], -SCALE, None, ALU.mult).then_inc(sm_step, 1)

            def weights(b, i):
                w, r = (i + 1) * P, i % 2
                dve.wait_ge(p_exp, b * TT + (i + 1))
                dve.reciprocal(rinv[:, r:r + 1], rsum[:, r:r + 1]).then_inc(p_norm, 1)
                dve.wait_ge(p_norm, b * (2 * TT) + (2 * i + 1))
                dve.tensor_scalar(prob[r][:, 0:w], prob[r][:, 0:w], rinv[:, r:r + 1], None, ALU.mult).then_inc(p_norm, 1)

            def attended(b, i):
                dve.wait_ge(o_full, b * TT + (i + 1))
                t = x1[:, :, i * P:(i + 1) * P]
                dve.tensor_tensor(t, t, banks(PO)[:, 0:C].rearrange("p (t n) -> p t n", t=CT),
                                  ALU.add).then_inc(x1_attn, 1)

            def each(ap):
                return ap.unsqueeze(2).broadcast_to([P, TT, NE])

            def gate(b):
                g0 = b * GATE_STEPS
                count = [0]

                def step(ins):
                    count[0] += 1
                    ins.then_inc(g_step, 1)
                    dve.wait_ge(g_step, g0 + count[0])

                dve.wait_ge(g_full, b + 1)
                step(dve.tensor_tensor(gs, banks(PO)[:, 0:TT * NE].rearrange("p (t e) -> p t e", e=NE),
                                       gb_sb[:].unsqueeze(1).broadcast_to([P, TT, NE]), ALU.add))
                step(dve.tensor_reduce(gr, gs, AX.X, ALU.max))
                step(dve.tensor_tensor(gs, gs, each(gr), ALU.subtract))
                dve.wait_ge(g_exp, b + 1)
                step(dve.tensor_reduce(gr, gp, AX.X, ALU.add))
                step(dve.reciprocal(gi, gr))
                step(dve.tensor_tensor(gp, gp, each(gi), ALU.mult))
                other = gp.unsqueeze(2).broadcast_to([P, TT, NE, NE])
                own = gp.unsqueeze(3).broadcast_to([P, TT, NE, NE])
                step(dve.tensor_tensor(cgt, other, own, ALU.is_gt))
                step(dve.tensor_tensor(ceq, other, own, ALU.is_equal))
                step(dve.tensor_tensor(ceq, ceq, low_sb[:].unsqueeze(1).broadcast_to([P, TT, NE, NE]), ALU.mult))
                step(dve.tensor_tensor(cgt, cgt, ceq, ALU.add))
                step(dve.tensor_reduce(rank, cgt, AX.X, ALU.add))
                step(dve.scalar_tensor_tensor(out=gp, in0=rank, scalar=1.5, in1=gp, op0=ALU.is_lt, op1=ALU.mult))
                step(dve.tensor_reduce(gr, gp, AX.X, ALU.add))
                step(dve.tensor_scalar(gr, gr, 1e-9, None, ALU.add))
                assert count[0] == GATE_STEPS, count
                dve.reciprocal(gi, gr).then_inc(g_norm, 1)
                dve.wait_ge(g_norm, b * 2 + 1)
                dve.tensor_tensor(gp, gp, each(gi), ALU.mult).then_inc(g_norm, 1)

            def second_biases(b):
                for i in range(CT * NH):
                    dve.wait_ge(b2_full, b * (CT * NH) + (i + 1))
                    t = x1[:, i // NH, (i % NH) * HALF:(i % NH + 1) * HALF]
                    dve.tensor_tensor(t, t, banks(PH + i % 5), ALU.add).then_inc(b2_add, 1)

            def expert_out(b, ec, chunk):
                g = b * E_B + ec
                dve.wait_ge(pair_used, g * PAIRS + (PAIRS + RING))
                dve.wait_ge(gbc_copy, g + 1)
                dve.wait_ge(x1_ffn, g + 1)
                dve.tensor_tensor(ytmp[:], banks(PY, CT).rearrange("p (t n) -> p t n", t=CT),
                                  gbc[:].unsqueeze(1).broadcast_to([P, CT, HALF]), ALU.mult).then_inc(y_read, 1)
                dve.wait_ge(y_read, g + 2)
                t = x1[:, :, chunk * HALF:(chunk + 1) * HALF]
                dve.tensor_tensor(t, t, ytmp[:], ALU.add).then_inc(x1_ffn, 1)

            def side(b, m, part, scan=True):
                i = m - T_TILE
                if part == 0 and m == T_NORM:
                    norm_centre(b * 3 + 1, x1, xln, PY)
                if part == 0 and m == T_GATE:
                    norm_centre(b * 3 + 2, x1, xln, PY)
                if part == 1:
                    if 0 <= i < TT:
                        maximum(b, i)
                    if m == 0:
                        dve.wait_ge(out_done, b * 16 + 1)
                        norm_centre(b * 3, acc, x1, PY)
                        if scan:
                            dve.wait_ge(ln_cent, b * (3 * NH) + NH)
                            start_sum(b + 1)
                if part == 2:
                    if m == 1:
                        norm_scale(b * 3, x1, scan_rstd)
                    if m == 2:
                        scan_residual(b)
                    if m == T_NORM:
                        norm_scale(b * 3 + 1, xln, rstd)
                    if 0 <= i < TT:
                        weights(b, i)
                    if 1 <= i <= TT:
                        attended(b, i - 1)
                    if m == T_GATE:
                        norm_scale(b * 3 + 2, xln, rstd)
                    if m == T_GATE + 1:
                        gate(b)
                    if m == T_GATE + 3:
                        second_biases(b)

            def experts(b, m):
                for q in pairs_at(m):
                    if q > PAIRS and q % PAIRS == 1:
                        expert_out(b, q // PAIRS - 1, (q // PAIRS - 1) % NH)

            def beside(b):
                for k in range(K):
                    for n in range(N):
                        m = k * N + n
                        if m < SIDE:
                            slot(b, k, n, lambda part: side(b - 1, m, part))
                        else:
                            slot(b, k, n, lambda part: experts(b - 1, m) if part == 0 else None)
                    if following(b, k):
                        inputs(*following(b, k), 0, True)
                expert_out(b - 1, E_B - 1, NH - 1)

            channel_stats(0, u)
            spread(0)
            norm_image(0, u)
            start_sum(0)
            split_rows(0, 0)
            for j in range(CT):
                correction(0, 0, j)
            steps(0, 0)
            inputs(0, 0, 0, True)
            for k in range(K):
                scans(0, k, 0)
                inputs(0, k, 1)
                with dve.Fori(1, AHEAD) as n:
                    scans(0, k, n, True)
                    inputs(0, k, n + 1)
                for n in range(AHEAD, N):
                    slot(0, k, n, lambda part: None)
                inputs(*following(0, k), 0, True)
            with dve.Fori(1, NB - 1) as b:
                beside(b)
            beside(NB - 1)
            for m in range(SIDE):
                for part in range(3):
                    side(NB - 1, m, part, False)
            with dve.Fori(0, NE) as e:
                for chunk in range(NH):
                    expert_out(NB - 1, e * NH + chunk, chunk)

        @block.tensor
        def _(pe):
            pe.wait_ge(c_load, 16 * CONST_LOADS)

            def over_channels(bank, src, s):
                for j in range(CT):
                    mm = pe.matmul(banks(bank + s), mean_w[:], src[:, j, s * HALF:(s + 1) * HALF],
                                   start=(j == 0), stop=(j == CT - 1))
                return mm

            def norm_mean(bank, src):
                for s in range(NH):
                    over_channels(bank, src, s).then_inc(ln_mean, 1)

            def norm_var(c, sq):
                for s in range(NH):
                    pe.wait_ge(ln_sq, c * NH + (s + 1))
                    over_channels(PH, sq, s).then_inc(ln_var, 1)

            def group_sums(b, stat):
                if stat == 0:
                    pe.wait_ge(gm_full, b * 16 + 16)
                pe.wait_ge(gn_step, b * GN_STEPS + (9, GN_STEPS)[stat])
                pe.wait_ge(misc_free, sums_use(b, stat) + 1)
                for o in range(CT):
                    near = [j for j in range(CT) if (j, o) in BLOCKS]
                    for j in near:
                        mm = pe.matmul(banks(PM)[:, o:o + 1], gm_w[:, BLOCKS.index((j, o)), :],
                                       mv[:, j, stat:stat + 1], start=(j == near[0]), stop=(j == near[-1]))
                mm.then_inc(misc_full, 1)

            def make_rows(b, k, s):
                if k == 0:
                    pe.wait_ge(u_ready, b * CT + CT)
                pe.wait_ge(misc_free, rows_use(b, k, s) + 1)
                for j in range(CT):
                    mm = pe.matmul(banks(PM)[0:3 * BC + R, :], xpw_sb[:, j, k, :],
                                   u[:, j, s * HALF:(s + 1) * HALF], start=(j == 0), stop=(j == CT - 1))
                mm.then_inc(misc_full, 1)

            def step_tile(b, k, j):
                kk = b * K + k
                if j == 0:
                    pe.wait_ge(misc_free, rows_use(b, k, NH - 1) + 2)
                    pe.wait_ge(dbu_done, kk * (N * CT) + 1)
                else:
                    pe.wait_ge(dt_read, kk * CT + j)
                for s in range(NH):
                    mm = pe.matmul(banks(PB + s), dtw_sb[:, k, j * P:(j + 1) * P],
                                   xd[3 * BC:3 * BC + R, s * HALF:(s + 1) * HALF], start=True, stop=True)
                mm.then_inc(dt_full, 1)

            def b_row(b, k, n):
                kk = b * K + k
                S = bcs[0:3 * BC, k % 2, :]
                pe.wait_ge(split_step, kk * SPLIT_STEPS + (SPLIT_STEPS + 1))
                if isinstance(n, int) and n == 0:
                    pe.wait_ge(dt_read, kk * CT + CT)
                else:
                    pe.wait_ge(dbu_done, (kk * N + n) * CT + 1)
                for s in range(NH):
                    mm = pe.matmul(banks(PB + s), sel[0:3 * BC, bass.ds(n, 1), :].rearrange("p a n -> p (a n)"),
                                   S[:, s * HALF:(s + 1) * HALF], start=True, stop=True)
                mm.then_inc(b_full, 1)

            def c_half(b, k, n, s):
                pe.wait_ge(misc_free, c_use(b, k, n) + (s + 1))
                pe.matmul(banks(PM), sel[0:3 * BC, bass.ds(n + N, 1), :].rearrange("p a n -> p (a n)"),
                          bcs[0:3 * BC, k % 2, s * HALF:(s + 1) * HALF], start=True, stop=True).then_inc(misc_full, 1)

            def state_rows(b, k, n):
                b_row(b, k, n)
                c_half(b, k, n, 0)
                c_half(b, k, n, 1)

            def start_sum():
                pe.wait_ge(acc_init, SUM_PE)
                for j in range(SUM_PE):
                    for s in range(NH):
                        pe.matmul(banks(PH + j * NH + s), ident[:], acc[:, j, s * HALF:(s + 1) * HALF],
                                  start=True, stop=False)

            def sum_state(k, n):
                g, last = k * N + n, k == K - 1 and is_int(n, N - 1)
                for j in range(SUM_PE):
                    pe.wait_ge(hc_done, g * CT + (j + 2))
                    for s in range(NH):
                        mm = pe.matmul(banks(PH + j * NH + s), ident[:],
                                       by_rows(h[:, j, :], k)[:, s * (HH // NH):(s + 1) * (HH // NH), :],
                                       start=False, stop=last)
                    mm.then_inc(acc_pe, 1)

            def next_direction(b, k, n):
                after = following(b, k)
                if after and n - AHEAD in range(NH):
                    make_rows(*after, n - AHEAD)
                if k == GN_K and not is_int(b, NB - 1):
                    if n == AHEAD + 2:
                        group_sums(b + 1, 0)
                    if n == AHEAD + 3:
                        group_sums(b + 1, 1)
                if after and n == N - 2:
                    step_tile(*after, 0)

            def before_slot(b, k, n):
                if n < N - 1:
                    b_row(b, k, n + 1)
                elif following(b, k):
                    step_tile(*following(b, k), 1)

            def between(b, k, n, s0=0, s1=NH):
                if n < N - 1:
                    for s in range(s0, s1):
                        c_half(b, k, n + 1, s)
                elif following(b, k):
                    step_tile(*following(b, k), 2)
                    state_rows(*following(b, k), 0)

            def kv_groups(b, i0, i1):
                for i in range(i0, i1):
                    if i >= 2:
                        pe.wait_ge(kv_copy, b * KV + (i - 1))
                    for c in range(CT):
                        if i < TT:
                            mm = pe.matmul(banks(PH + i % 2)[:, 0:C], xln[:, c, i * P:(i + 1) * P],
                                           wq_sb[:, c, 2, :], start=(c == 0), stop=(c == CT - 1))
                        else:
                            o, s = (i - TT) // NH, (i - TT) % NH
                            mm = pe.matmul(banks(PH + i % 2), wq_sb[:, c, 1, o * P:(o + 1) * P],
                                           xln[:, c, s * HALF:(s + 1) * HALF], start=(c == 0), stop=(c == CT - 1))
                    mm.then_inc(kv_full, 1)

            def q_tile(b, i):
                if i >= 3:
                    pe.wait_ge(x1_attn, b * TT + (i - 2))
                for o in range(CT):
                    for c in range(CT):
                        mm = pe.matmul(banks(PO)[:, o * P:(o + 1) * P], wq_sb[:, c, 0, o * P:(o + 1) * P],
                                       xln[:, c, i * P:(i + 1) * P], start=(c == 0), stop=(c == CT - 1))
                mm.then_inc(q_full, 1)

            def scores(b, i):
                w = (i + 1) * P
                if i == 0:
                    pe.wait_ge(kv_copy, b * KV + KV)
                else:
                    pe.wait_ge(p_exp, b * TT + i)
                pe.wait_ge(q_copy, b * TT + (i + 1))
                for a in range(0, w, HALF):
                    z = min(w, a + HALF)
                    for c in range(CT):
                        mm = pe.matmul(banks(PY, 2)[:, a:z], qt[:, c, :], kt[:, c, a:z],
                                       start=(c == 0), stop=(c == CT - 1))
                mm.then_inc(s_full, 1)

            def turn(b, i):
                pe.wait_ge(p_norm, b * (2 * TT) + (2 * i + 2))
                for s in range(i + 1):
                    mm = pe.transpose(banks(PH, 2)[:, s * P:(s + 1) * P], prob[i % 2][:, s * P:(s + 1) * P], ident[:])
                mm.then_inc(pt_full, 1)

            def attend(b, i):
                if i >= 1:
                    pe.wait_ge(x1_attn, b * TT + i)
                pe.wait_ge(q_copy, b * TT + min(i + 3, TT))
                pe.wait_ge(pt_copy, b * TT + (i + 1))
                for o in range(CT):
                    for s in range(i + 1):
                        mm = pe.matmul(banks(PO)[:, o * P:(o + 1) * P], vv[:, s, o * P:(o + 1) * P],
                                       pt[:, s * P:(s + 1) * P], start=(s == 0), stop=(s == i))
                mm.then_inc(o_full, 1)

            def gate_scores(b):
                pe.wait_ge(ln_out, b * (3 * NH) + 3 * NH)
                for t in range(TT):
                    for c in range(CT):
                        mm = pe.matmul(banks(PO)[:, t * NE:(t + 1) * NE], xln[:, c, t * P:(t + 1) * P], gw_sb[:, c, :],
                                       start=(c == 0), stop=(c == CT - 1))
                mm.then_inc(g_full, 1)

            def gate_turn(b):
                pe.wait_ge(g_norm, b * 2 + 2)
                for t in range(TT):
                    mm = pe.transpose(banks(PY, 2)[0:NE, t * P:(t + 1) * P], gp[:, t, :], ident[:])
                mm.then_inc(g_turn, 1)

            def second_biases(b):
                pe.wait_ge(g_copy, b + 1)
                pe.wait_ge(b2_load, b * 16 + 16)
                for i in range(CT * NH):
                    if i == 5:
                        pe.wait_ge(b2_add, b * (CT * NH) + 1)
                    pe.matmul(banks(PH + i % 5), b2_sb[:, i // NH * P:(i // NH + 1) * P],
                              gt[:, (i % NH) * HALF:(i % NH + 1) * HALF], start=True, stop=True).then_inc(b2_full, 1)

            def side(b, m, score=True):
                if m == 0:
                    pe.wait_ge(acc_done, b * (K * N * CT) + (K * N * CT + CT))
                    pe.wait_ge(y_read, b * E_B + 1)
                    norm_mean(PY, acc)
                if m == 1:
                    norm_var(b * 3, tmp)
                if m == T_NORM - 1:
                    pe.wait_ge(x1_ssm, b * CT + (CT + 1))
                    norm_mean(PY, x1)
                if m == T_NORM:
                    norm_var(b * 3 + 1, tmp)
                if m == T_KV:
                    pe.wait_ge(wq_full, b * 16 + 16)
                    pe.wait_ge(ln_out, b * (3 * NH) + 2 * NH)
                if T_KV <= m < T_TILE:
                    kv_groups(b, *kv_part(m))
                i = m - T_TILE
                if 0 <= i < TT and score:
                    scores(b, i)
                if 0 <= i + 1 < TT:
                    q_tile(b, i + 1)
                if 1 <= i <= TT:
                    turn(b, i - 1)
                    attend(b, i - 1)
                if m == T_GATE - 1:
                    pe.wait_ge(x1_attn, b * TT + TT)
                    norm_mean(PY, x1)
                if m == T_GATE:
                    norm_var(b * 3 + 2, spare)
                if m == T_GATE + 1:
                    gate_scores(b)
                if m == T_GATE + 2:
                    gate_turn(b)
                if m == T_GATE + 3:
                    second_biases(b)

            def expert_step(b, e, chunk, p, lag, slot=None):
                ec = (b * NE + e) * NH + chunk
                cols = slice(chunk * HALF, (chunk + 1) * HALF)
                w1 = ring[:, p % RING, 0:CT * 2 * P].rearrange("p (t n) -> p t n", t=CT)
                pe.wait_ge(w_full[p % RING], ec * (16 * PAIRS // RING) + 16 * (p // RING + 1))
                pe.wait_ge(gelu_done, ec * (2 * PAIRS) + (2 * p + 1))
                for s in range(2):
                    for c in range(CT):
                        mm = pe.matmul(banks(PH + s), w1[:, c, s * P:(s + 1) * P], xln[:, c, cols],
                                       start=(c == 0), stop=(c == CT - 1))
                    mm.then_inc(l1_full, 1)
                split = slot and slot[2] < N - 1
                if slot:
                    between(*slot, 0, NH // 2 if split else NH)
                inner = (lambda: between(*slot, NH // 2, NH)) if split else None
                if p == 1:
                    pe.wait_ge(y_read, ec + 1)
                    if chunk == 0:
                        pe.wait_ge(sel_copy, b * NE + (e + 1))
                    pe.matmul(banks(PY + CT - 1), selc, gt[:, cols], start=True, stop=True).then_inc(gbc_full, 1)
                if p == 0:
                    if lag:
                        expert_second(ec - 1, PAIRS - 1, inner)
                    elif inner:
                        inner()
                else:
                    expert_second(ec, p - 1, inner)

            def expert_second(ec, p, inner=None):
                w2 = ring[:, p % RING, CT * 2 * P:].rearrange("p (t n) -> p t n", t=2)
                pe.wait_ge(gelu_done, ec * (2 * PAIRS) + (2 * p + 3))
                for o in range(CT):
                    if p == 0 and o == CT - 1:
                        pe.wait_ge(gbc_copy, ec + 1)
                    for s in range(2):
                        mm = pe.matmul(banks(PY + o), w2[:, s, o * P:(o + 1) * P], hid[:, p % 2, s, :],
                                       start=(p == 0 and s == 0), stop=(p == PAIRS - 1 and s == 1))
                    if o == 0 and inner:
                        inner()
                mm.then_inc(pair_used, 1)

            def beside(b):
                for k in range(K):
                    for n in range(N):
                        m = k * N + n
                        before_slot(b, k, n)
                        if m < SIDE:
                            split = n < N - 2 and 0 < m - T_TILE < TT
                            between(b, k, n, 0, NH // 2 if split else NH)
                            if split:
                                scores(b - 1, m - T_TILE)
                                between(b, k, n, NH // 2, NH)
                            if n < N - 2:
                                next_direction(b, k, n)
                            side(b - 1, m, not split)
                            if n == N - 2:
                                next_direction(b, k, n)
                            continue
                        for i, q in enumerate(pairs_at(m)):
                            if q == 0:
                                pe.wait_ge(b2_add, (b - 1) * (CT * NH) + CT * NH)
                            expert_step(b - 1, q // (NH * PAIRS), q // PAIRS % NH, q % PAIRS, q > 0,
                                        (b, k, n) if i == 0 else None)
                        next_direction(b, k, n)
                expert_second((b - 1) * E_B + (E_B - 1), PAIRS - 1)

            group_sums(0, 0)
            group_sums(0, 1)
            make_rows(0, 0, 0)
            make_rows(0, 0, 1)
            for j in range(CT):
                step_tile(0, 0, j)
            pe.wait_ge(c_pool, 6)
            state_rows(0, 0, 0)
            start_sum()
            for k in range(K):
                with pe.Fori(0, AHEAD) as n:
                    state_rows(0, k, n + 1)
                    sum_state(k, n)
                for n in range(AHEAD, N):
                    before_slot(0, k, n)
                    between(0, k, n)
                    sum_state(k, n)
                    next_direction(0, k, n)
            with pe.Fori(1, NB - 1) as b:
                beside(b)
            beside(NB - 1)
            for m in range(SIDE):
                side(NB - 1, m)
            pe.wait_ge(b2_add, NB * CT * NH)

            def expert(e):
                for chunk in range(NH):
                    for p in range(PAIRS):
                        expert_step(NB - 1, e, chunk, p, not (is_int(e, 0) and chunk + p == 0))

            expert(0)
            with pe.Fori(1, NE) as e:
                expert(e)
            expert_second(NB * E_B - 1, PAIRS - 1)


_INS = ["x", "xpw", "dtw", "chan", "wqkv", "gate_w", "gate_b", "b1", "b2", "wpk", "gmat", "lower"]


def kernel(**inputs):
    import numpy as np
    import concourse.bacc as bacc
    from concourse.bass_utils import run_bass_kernel_spmd

    a = {k: np.ascontiguousarray(v) for k, v in inputs.items()}
    proj = a["L0_conv_x_proj_weight"].transpose(2, 0, 1)
    rows = proj[:, :, R:]
    per_channel = [a["L0_conv_dt_projs_bias"].T,
                   a["L0_conv_A_logs"].reshape(K, C, N).transpose(1, 0, 2).reshape(C, K * N),
                   a["L0_conv_Ds"].reshape(K, C).T, a["L0_conv_ln_weight"][:, None], a["L0_conv_ln_bias"][:, None]]
    w1 = a["L1_ffn_w1"].reshape(NE, CT, P, PAIRS, 2 * P).transpose(0, 3, 2, 1, 4).reshape(NE * PAIRS, P, CT * 2 * P)
    w2 = a["L1_ffn_w2"].reshape(NE, PAIRS, 2, P, C).transpose(0, 1, 3, 2, 4).reshape(NE * PAIRS, P, 2 * C)
    groups = np.arange(C) // GROUP
    gmat = (groups[:, None] == groups[None]).astype(np.float32) / np.float32(GROUP)
    data = {
        "x": a["x"].reshape(NB, C, L),
        "xpw": np.concatenate([rows, rows, rows, proj[:, :, :R]], axis=2),
        "dtw": a["L0_conv_dt_projs_weight"].transpose(2, 0, 1),
        "chan": np.concatenate(per_channel, axis=1),
        "wqkv": np.stack([a["L1_attn_Wq"], a["L1_attn_Wk"], a["L1_attn_Wv"]], axis=1),
        "gate_w": a["L1_ffn_gate_w"],
        "gate_b": np.repeat(a["L1_ffn_gate_b"][None], P, axis=0),
        "b1": a["L1_ffn_b1"].reshape(NE, 2 * PAIRS, P).transpose(2, 0, 1).reshape(P, NE * 2 * PAIRS),
        "b2": a["L1_ffn_b2"],
        "wpk": np.concatenate([w1, w2], axis=2),
        "gmat": np.stack([gmat[j * P:(j + 1) * P, o * P:(o + 1) * P]
                          for j in range(CT) for o in range(CT) if abs(j - o) <= 1]),
        "lower": np.repeat(np.tril(np.ones((NE, NE), np.float32), -1)[None], P, axis=0),
    }
    nc = bacc.Bacc("TRN2", target_bir_lowering=False, num_devices=1)
    arrays, aps = {}, []
    for name in _INS:
        arr = np.ascontiguousarray(data[name])
        arrays[f"in_{name}"] = arr
        aps.append(nc.dram_tensor(f"in_{name}", arr.shape, mybir.dt.from_np(arr.dtype), kind="ExternalInput").ap())
    out = nc.dram_tensor("out_0", (NB, C, L), F32, kind="ExternalOutput").ap()
    build(nc, *aps, out)
    r = run_bass_kernel_spmd(nc, [arrays], core_ids=[0])
    return r.results[0]["out_0"].reshape(NB, C, HH, WW)
```
